# Optimizing a Trainium2 kernel written in Bass

```python
import numpy as np
import jax
import jax.numpy as jnp

def _softmax(x, axis=-1):
    return jax.nn.softmax(x, axis=axis)

def _gelu(x):
    return jax.nn.gelu(x, approximate=True)

def _silu(x):
    return jax.nn.silu(x)

def _sigmoid(x):
    return jax.nn.sigmoid(x)

def _layernorm(x, axis=-1, eps=1e-05):
    m = jnp.mean(x, axis=axis, keepdims=True)
    v = jnp.var(x, axis=axis, keepdims=True)
    return (x - m) / jnp.sqrt(v + eps)

def _scatter_add(tgt, idx, src, axis=0):
    return tgt.at[idx].add(src)

def _segment_sum(src, seg, n):
    return jax.ops.segment_sum(src, seg, n)
kernel_name = 'mk_gnn_preln_d2_gnn_r8_5cfd81'

def setup_inputs(seed: int=0):
    np.random.seed(seed)
    _w = jnp.asarray

    def _rec_inputs():
        import jax
        import jax.numpy as jnp
        _gk = jax.random.key(seed)
        x = -0.0003713 + 1 * jax.random.normal(jax.random.fold_in(_gk, 1), (6250, 128), jnp.float32)
        _s = jax.random.randint(jax.random.fold_in(_gk, 2), (100000,), 0, 6250, jnp.int32)
        _d = jax.random.randint(jax.random.fold_in(_gk, 3), (100000,), 0, 6250, jnp.int32)
        _loop = jnp.arange(6250, dtype=jnp.int32)
        src = jnp.concatenate([_s, _d, _loop])
        dst = jnp.concatenate([_d, _s, _loop])
        _o = jnp.argsort(dst, stable=True)
        src = src[_o]
        dst = dst[_o]
        edge_attr_128 = -2.25437e-05 + 0.999858 * jax.random.normal(jax.random.fold_in(_gk, 11), (206250, 128), jnp.float32)
        edge_weight = jax.random.uniform(jax.random.fold_in(_gk, 14), (206250,), jnp.float32, 0.0, 0.999999)
        return (x, src, dst, edge_attr_128, edge_weight)
    x, src, dst, edge_attr_128, edge_weight = _rec_inputs()

    def _L0_gnn_setup():
        import jax, jax.numpy as jnp
        import numpy as np
        N = 12500
        E = 200000
        F = 128
        U = 128
        key = jax.random.key(seed)
        k1, k2, k3, k4 = jax.random.split(key, 4)
        x = jax.random.normal(k1, (N, F), dtype=jnp.float32)
        edge_index = jax.random.randint(k2, (2, E), 0, N, dtype=jnp.int32)
        edge_weight = jax.random.uniform(k3, (E,), dtype=jnp.float32)
        glorot = (2.0 / (F + U)) ** 0.5
        kernel = jax.random.normal(k4, (F, U), dtype=jnp.float32) * glorot
        bias = jnp.zeros((U,), dtype=jnp.float32)
        return {'x': x, 'edge_index': edge_index, 'edge_weight': edge_weight, 'kernel': kernel, 'bias': bias}
    _L0_gnn_all = _L0_gnn_setup()
    _L0_gnn_in = {k: v for k, v in _L0_gnn_all.items() if k in ('kernel', 'bias')}
    del _L0_gnn_all

    def _L1_gnn_setup():
        import jax, jax.numpy as jnp
        import numpy as np
        N_NODES = 6250
        N_EDGES = 62500
        D = 128
        LEAKY_SLOPE = 0.01
        LN_EPS = 1e-05
        AGG_EPS = 1e-07
        key = jax.random.key(seed)
        ks = jax.random.split(key, 6)
        scale = 1.0 / np.sqrt(2 * D)
        return {'H': jax.random.normal(ks[0], (N_NODES, D), dtype=jnp.float32), 'E': jax.random.normal(ks[1], (N_EDGES, D), dtype=jnp.float32), 'ht': jax.random.randint(ks[2], (N_EDGES, 2), 0, N_NODES, dtype=jnp.int32), 'W_fwd': jax.random.normal(ks[3], (2 * D, D), dtype=jnp.float32) * scale, 'b_fwd': jnp.zeros((D,), dtype=jnp.float32), 'W_back': jax.random.normal(ks[4], (2 * D, D), dtype=jnp.float32) * scale, 'b_back': jnp.zeros((D,), dtype=jnp.float32), 'gamma': jnp.ones((D,), dtype=jnp.float32), 'beta': jnp.zeros((D,), dtype=jnp.float32)}
    _L1_gnn_all = _L1_gnn_setup()
    _L1_gnn_in = {k: v for k, v in _L1_gnn_all.items() if k in ('W_fwd', 'b_fwd', 'W_back', 'b_back', 'gamma', 'beta')}
    del _L1_gnn_all
    return {'x': x, 'src': src, 'dst': dst, 'edge_attr_128': edge_attr_128, 'edge_weight': edge_weight, 'L0_gnn_kernel': _L0_gnn_in['kernel'], 'L0_gnn_bias': _L0_gnn_in['bias'], 'L1_gnn_W_fwd': _L1_gnn_in['W_fwd'], 'L1_gnn_b_fwd': _L1_gnn_in['b_fwd'], 'L1_gnn_W_back': _L1_gnn_in['W_back'], 'L1_gnn_b_back': _L1_gnn_in['b_back'], 'L1_gnn_gamma': _L1_gnn_in['gamma'], 'L1_gnn_beta': _L1_gnn_in['beta']}

def reference(x, src, dst, edge_attr_128, edge_weight, L0_gnn_kernel, L0_gnn_bias, L1_gnn_W_fwd, L1_gnn_b_fwd, L1_gnn_W_back, L1_gnn_b_back, L1_gnn_gamma, L1_gnn_beta):
    import jax
    import jax.numpy as jnp

    def _L0_gnn_ref(x, edge_index, edge_weight, kernel, bias):
        import jax, jax.numpy as jnp
        import numpy as np
        N = 12500
        E = 200000
        F = 128
        U = 128
        num_nodes = x.shape[0]
        row, col = (edge_index[0], edge_index[1])
        loop_idx = jnp.arange(num_nodes, dtype=edge_index.dtype)
        row = jnp.concatenate([row, loop_idx])
        col = jnp.concatenate([col, loop_idx])
        w = jnp.concatenate([edge_weight, jnp.ones((num_nodes,), dtype=edge_weight.dtype)])
        deg = jax.ops.segment_sum(w, row, num_segments=num_nodes)
        dinv = jnp.where(deg > 0, jax.lax.rsqrt(deg), 0.0)
        w_norm = dinv[row] * w * dinv[col]
        h = x @ kernel
        msg = w_norm[:, None] * h[col]
        out = jax.ops.segment_sum(msg, row, num_segments=num_nodes)
        return jax.nn.relu(out + bias)

    def _L1_gnn_ref(H, E, ht, W_fwd, b_fwd, W_back, b_back, gamma, beta):
        import jax, jax.numpy as jnp
        import numpy as np
        N_NODES = 6250
        N_EDGES = 62500
        D = 128
        LEAKY_SLOPE = 0.01
        LN_EPS = 1e-05
        AGG_EPS = 1e-07
        n = H.shape[0]
        heads = ht[:, 0]
        tails = ht[:, 1]
        msg_fwd = jnp.concatenate([H[heads], E], axis=1) @ W_fwd + b_fwd
        msg_back = jnp.concatenate([H[tails], E], axis=1) @ W_back + b_back
        msg_dst = jnp.concatenate([tails, heads])
        messages = jnp.concatenate([msg_fwd, msg_back], axis=0)
        agg = jax.ops.segment_sum(messages, msg_dst, num_segments=n)
        cnt = jax.ops.segment_sum(jnp.ones(msg_dst.shape, H.dtype), msg_dst, num_segments=n)
        agg = agg / (cnt[:, None] + AGG_EPS)
        x = jnp.where(agg >= 0, agg, LEAKY_SLOPE * agg) + H
        mu = jnp.mean(x, axis=-1, keepdims=True)
        var = jnp.mean(jnp.square(x - mu), axis=-1, keepdims=True)
        return gamma * (x - mu) * jax.lax.rsqrt(var + LN_EPS) + beta
    edge_index = jnp.stack([src, dst])
    edge_index_t = jnp.stack([src, dst], axis=1)
    h = jnp.maximum(_layernorm(x, axis=-1), 0.0)
    x = x + _L0_gnn_ref(h, edge_index, edge_weight, L0_gnn_kernel, L0_gnn_bias)
    h = jnp.maximum(_layernorm(x, axis=-1), 0.0)
    x = x + _L1_gnn_ref(h, edge_attr_128, edge_index_t, L1_gnn_W_fwd, L1_gnn_b_fwd, L1_gnn_W_back, L1_gnn_b_back, L1_gnn_gamma, L1_gnn_beta)
    return x

_drawn_inputs = setup_inputs


def setup_inputs(seed=0):
    import zlib

    import numpy as np

    out = dict(_drawn_inputs(seed))
    spreads = {'L0_gnn_bias': (0.0, 0.1),
     'L1_gnn_b_fwd': (0.0, 0.268),
     'L1_gnn_b_back': (0.0, 0.1),
     'L1_gnn_gamma': (1.0, 0.2),
     'L1_gnn_beta': (0.0, 0.1)}
    factors = {}
    for name, (base, spread) in spreads.items():
        noise = np.random.default_rng([zlib.crc32(name.encode()), seed]).standard_normal(out[name].shape)
        drawn = base * np.exp(spread * noise) if base else spread * noise
        out[name] = jnp.asarray(drawn.astype(out[name].dtype))
    for name, factor in factors.items():
        out[name] = (out[name] * factor).astype(out[name].dtype)
    return out
```

```python
from contextlib import ExitStack

import numpy as np
import concourse.bass as bass
from concourse import mybir

F32 = mybir.dt.float32
I32 = mybir.dt.int32
ALU = mybir.AluOpType
ACT = mybir.ActivationFunctionType
AX_X = mybir.AxisListType.X

N = 6250
E = 206250
F = 128
P = 128
NP, NT = 125, 50
J = 8
GE = P * J
NG = 2 * -(-E // (2 * GE))
EP = NG * GE
FULL = E // GE
TAILP, TAILJ = divmod(E - FULL * GE, J)
PADKEY = N
SPARE = N + 1
ROWS = 6400
K = 4
LN_EPS = 1e-5
AGG_EPS = 1e-7
SLOPE = 0.01
ROUND = 12582912.0


def semaphores(nc, ctx, prefix):
    taken = []

    def sem(name):
        taken.append(nc.alloc_semaphore(prefix + name))
        return taken[-1]

    def clear():
        nc.clear_and_free_semaphores(taken)
        nc.all_engine_barrier()

    ctx.callback(clear)
    return sem


class Net:
    pass


def setup_and_degrees(nc, d):
    with ExitStack() as ctx:
        sb = lambda name, shape, dt=F32: ctx.enter_context(nc.sbuf_tensor(name, shape, dt))
        sem = semaphores(nc, ctx, "setup_")
        src_i = sb("src_i", [P, NG, J], I32)
        dst_i = sb("dst_i", [P, NG, J], I32)
        src_f = sb("src_f", [P, NG, J])
        dst_f = sb("dst_f", [P, NG, J])
        w = sb("w_all", [P, NG, J])
        row_of = sb("row_of", [P, NG, J])
        col_of = sb("col_of", [P, NG, J])
        iota_i = sb("iota_i", [P, P], I32)
        iota = sb("iota", [P, P])
        row_hot = sb("row_hot", [P, 2, J, NP])
        col_hot = sb("col_hot", [P, 2, J, NT])
        deg = sb("deg", [NP, NT])
        has_edge = sb("has_edge", [NP, NT])
        x = sb("x_sb", [NP, NT, F])
        xc = sb("xc", [NP, NT, F])
        stat = sb("stat", [NP, 4, NT])
        hist = d.bank[0:2]
        edges_in = sem("edges_in")
        x_in = sem("x_in")
        pads = sem("pads")
        iota_ready = sem("iota_ready")
        done = sem("setup_dve")
        pad_ready = sem("pad_ready")
        var_ready = sem("var_ready")
        std_ready = sem("std_ready")
        g_ready = sem("g_ready")
        hot_ready = sem("hot_ready")
        hist_ready = sem("hist_ready")
        hist_used = sem("hist_used")
        stored = sem("setup_stored")
        block = ctx.enter_context(nc.Block())

        @block.sync
        def _(sp):
            sp.dma_start(x[:], d.x.rearrange("(p t) f -> p t f", p=NP)).then_inc(x_in, 16)
            sp.wait_ge(pads, 5)
            for a, t in ((d.src, src_i), (d.dst, dst_i), (d.w, w)):
                sp.dma_start(t[:, 0:FULL, :], a[0:FULL * GE].rearrange("(g p j) -> p g j", p=P, j=J)).then_inc(edges_in, 16)
                at = FULL * GE
                sp.dma_start(t[0:TAILP, FULL, :], a[at:at + TAILP * J].rearrange("(p j) -> p j", j=J)).then_inc(edges_in, 16)
                sp.dma_start(t[TAILP:TAILP + 1, FULL, 0:TAILJ], a[at + TAILP * J:E].rearrange("(p j) -> p j", p=1)).then_inc(edges_in, 16)
            sp.wait_ge(pad_ready, 1)
            for a, t in ((d.src_i, src_i), (d.dst_i, dst_i), (d.src_f, src_f), (d.dst_f, dst_f), (d.wp, w)):
                sp.dma_start(a.rearrange("(g p j) -> p g j", p=P, j=J), t[:]).then_inc(stored, 16)
            sp.wait_ge(g_ready, 1)
            sp.dma_start(d.g[0:N, :].rearrange("(p t) f -> p t f", p=NP), xc[:]).then_inc(stored, 16)
            sp.wait_ge(stored, 16 * 6)

        @block.gpsimd
        def _(pool):
            nc.gpsimd.iota(iota_i[:], pattern=[[1, P]], base=0, channel_multiplier=0).then_inc(iota_ready, 1)

        @block.scalar
        def _(act):
            act.wait_ge(var_ready, 1)
            nc.scalar.activation(stat[:, 2, :], stat[:, 1, :], ACT.Sqrt).then_inc(std_ready, 1)
            act.wait_ge(var_ready, 2)
            nc.scalar.activation(stat[:, 2, :], deg[:], ACT.Sqrt).then_inc(std_ready, 1)

        @block.vector
        def _(dve):
            count = [0]

            def link(ins):
                count[0] += 1
                ins.then_inc(done, 1)
                dve.wait_ge(done, count[0])

            nc.vector.memset(src_i[:, FULL:, :], PADKEY).then_inc(pads, 1)
            nc.vector.memset(dst_i[:, FULL:, :], PADKEY).then_inc(pads, 1)
            nc.vector.memset(w[:, FULL:, :], 0.0).then_inc(pads, 1)
            nc.vector.memset(deg[:], 1.0).then_inc(pads, 1)
            nc.vector.memset(stat[:, 3, :], 0.0).then_inc(pads, 1)
            dve.wait_ge(iota_ready, 1)
            link(nc.vector.tensor_copy(iota[:], iota_i[:]))
            dve.wait_ge(edges_in, 16 * 9)
            nc.vector.tensor_copy(src_f[:], src_i[:])
            link(nc.vector.tensor_copy(dst_f[:], dst_i[:]))
            link(nc.vector.tensor_scalar(row_of[:], src_f[:], 1.0 / NT, 0.5 / NT - 0.5, ALU.mult, ALU.add))
            link(nc.vector.tensor_scalar(row_of[:], row_of[:], ROUND, ROUND, ALU.add, ALU.subtract))
            ins = nc.vector.scalar_tensor_tensor(col_of[:], row_of[:], -float(NT), src_f[:], ALU.mult, ALU.add)
            link(ins)
            nc.vector.memset(stat[:, 3, :], 0.0).then_inc(pad_ready, 1)

            dve.wait_ge(x_in, 16)
            link(nc.vector.reduce_sum(stat[:, 0, :], x[:], AX_X))
            link(nc.vector.tensor_scalar(stat[:, 0, :], stat[:, 0, :], 1.0 / F, None, ALU.mult))
            link(nc.vector.tensor_tensor(xc[:], x[:], stat[:, 0, :].unsqueeze(2).to_broadcast([NP, NT, F]), ALU.subtract))
            link(nc.vector.tensor_tensor(x[:], xc[:], xc[:], ALU.mult))
            link(nc.vector.reduce_sum(stat[:, 1, :], x[:], AX_X))
            nc.vector.tensor_scalar(stat[:, 1, :], stat[:, 1, :], 1.0 / F, LN_EPS, ALU.mult, ALU.add).then_inc(var_ready, 1)
            dve.wait_ge(std_ready, 1)
            link(nc.vector.reciprocal(stat[:, 0, :], stat[:, 2, :]))
            link(nc.vector.tensor_tensor(xc[:], xc[:], stat[:, 0, :].unsqueeze(2).to_broadcast([NP, NT, F]), ALU.mult))
            link(nc.vector.tensor_scalar(xc[:], xc[:], 0.0, None, ALU.max))

            def one_hots(g, h):
                for j in range(J):
                    nc.vector.tensor_scalar(row_hot[:, h, j, :], iota[:, 0:NP], row_of[:, g, j:j + 1], None, ALU.is_equal)
                    last = nc.vector.tensor_scalar(col_hot[:, h, j, :], iota[:, 0:NT], col_of[:, g, j:j + 1],
                                                   w[:, g, j:j + 1], ALU.is_equal, ALU.mult)
                last.then_inc(hot_ready, 1)

            one_hots(0, 0)
            one_hots(1, 1)
            dve.wait_ge(hist_ready, 1)
            nc.vector.tensor_tensor(deg[:], deg[:], hist[0][0:NP, 0:NT], ALU.add).then_inc(hist_used, 1)
            with dve.Fori(1, NG // 2) as i:
                for h in range(2):
                    g = 2 * i + h
                    dve.wait_ge(hist_ready, g - 1)
                    one_hots(g, h)
                    dve.wait_ge(hist_ready, g)
                    dve.wait_ge(hist_used, g - 1)
                    nc.vector.tensor_tensor(deg[:], deg[:], hist[1 - h][0:NP, 0:NT], ALU.add).then_inc(hist_used, 1)
            dve.wait_ge(hist_ready, NG)
            dve.wait_ge(hist_used, NG - 1)
            link(nc.vector.tensor_tensor(deg[:], deg[:], hist[1][0:NP, 0:NT], ALU.add))

            link(nc.vector.tensor_scalar(has_edge[:], deg[:], 0.0, None, ALU.is_gt))
            nc.vector.tensor_scalar(deg[:], deg[:], 1e-30, None, ALU.max).then_inc(var_ready, 1)
            dve.wait_ge(std_ready, 2)
            link(nc.vector.reciprocal(stat[:, 0, :], stat[:, 2, :]))
            link(nc.vector.tensor_tensor(d.dinv[:], stat[:, 0, :], has_edge[:], ALU.mult))
            nc.vector.tensor_tensor(xc[:], xc[:], d.dinv[:].unsqueeze(2).to_broadcast([NP, NT, F]), ALU.mult).then_inc(g_ready, 1)

        @block.tensor
        def _(pe):
            def half(i, h, first):
                g = 2 * i + h
                pe.wait_ge(hot_ready, g + 1)
                if not first:
                    pe.wait_ge(hist_used, g - 1)
                for j in range(J):
                    last = nc.tensor.matmul(hist[h][0:NP, 0:NT], row_hot[:, h, j, :], col_hot[:, h, j, :],
                                            start=(j == 0), stop=(j == J - 1))
                last.then_inc(hist_ready, 1)

            half(0, 0, True)
            half(0, 1, True)
            with pe.Fori(1, NG // 2) as i:
                half(i, 0, False)
                half(i, 1, False)


def clear_tables(nc, sets):
    with ExitStack() as ctx:
        widest = max(t.shape[1] for t in sets)
        zeros = ctx.enter_context(nc.sbuf_tensor("zeros", [P, ROWS // P * widest], F32))
        sem = semaphores(nc, ctx, "clear_")
        zeroed, cleared = sem("zeroed"), sem("cleared")
        block = ctx.enter_context(nc.Block())

        @block.vector
        def _(dve):
            nc.vector.memset(zeros[:], 0.0).then_inc(zeroed, 1)

        @block.sync
        def _(sp):
            sp.wait_ge(zeroed, 1)
            for t in sets:
                sp.dma_start(t.rearrange("(p r) c -> p (r c)", p=P), zeros[:, 0:ROWS // P * t.shape[1]]).then_inc(cleared, 16)
            sp.wait_ge(cleared, 16 * len(sets))


def edge_pass(nc, d, name, rows_from, row_at, key, weight, edge_attr, tables):
    width = tables[0].shape[1]
    with ExitStack() as ctx:
        sb = lambda nm, shape, dt=F32: ctx.enter_context(nc.sbuf_tensor(f"{name}_{nm}", shape, dt))
        sem = semaphores(nc, ctx, name + "_")
        at_i = sb("at_i", [P, 2, J], I32)
        key_p = sb("key_p", [P, 2, J])
        key_b = sb("key_b", [P, 2, P, J])
        w_p = sb("w_p", [P, 2, J])
        attr = sb("attr", [P, 2, J, F])
        rows = sb("rows", [P, 2, J, F])
        same = sb("same", [P, 2, J, P])
        junk = sb("junk", [P, 2, J, P])
        before = sb("before", [P, 2, J])
        to_f = sb("to_f", [P, 2, J])
        to_i = sb("to_i", [P, 2, J], I32)
        sums = sb("sums", [P, 2, J, width])
        tri_i = sb("tri_i", [P, P], I32)
        lower = sb("lower", [P, P])
        spare_i = sb("spare_i", [P, J], I32)
        spare = sb("spare", [P, J])
        one = sb("one", [P, 1])
        bank = d.bank
        at_in = [sem(f"at_in{h}") for h in range(2)]
        key_in = [sem(f"key_in{h}") for h in range(2)]
        attr_in = [sem(f"attr_in{h}") for h in range(2)]
        tail_in = sem("tail_in")
        rows_in = [[sem(f"rows_in{h}_{j}") for j in range(J)] for h in range(2)]
        consts = sem("consts")
        ready = sem("ready")
        same_ready = sem("same_ready")
        to_ready = sem("to_ready")
        step = sem("step")
        summed = sem("summed")
        staged = sem("staged")
        turns = sem("turns")
        added = [sem(f"added{k}") for k in range(K)]
        per_table = J // K
        keys_dmas = 3 if weight is not None else 2
        block = ctx.enter_context(nc.Block())

        def loop(eng, half):
            half(0, 0, True)
            half(0, 1, True)
            with eng.Fori(1, NG // 2 - 1) as i:
                half(i, 0, False)
                half(i, 1, False)
            half(NG // 2 - 1, 0, False)
            half(NG // 2 - 1, 1, False)

        @block.sync
        def _(sp):
            def load(i, h, first, whole=True):
                g = 2 * i + h
                if not first:
                    sp.wait_ge(summed, J * (g - 1))
                    sp.wait_ge(to_ready, g - 1)
                at = slice(g * GE, (g + 1) * GE) if isinstance(g, int) else bass.ds(g * GE, GE)
                sp.dma_start(at_i[:, h, :], row_at[at].rearrange("(p j) -> p j", j=J)).then_inc(at_in[h], 16)
                sp.dma_start(key_p[:, h, :], key[at].rearrange("(p j) -> p j", j=J)).then_inc(key_in[h], 16)
                if weight is not None:
                    sp.dma_start(w_p[:, h, :], weight[at].rearrange("(p j) -> p j", j=J)).then_inc(key_in[h], 16)
                sp.dma_start(key_b[:, h, :, :].rearrange("p q j -> p (q j)"),
                             key[at].rearrange("(o e) -> o e", o=1).to_broadcast([P, GE])).then_inc(key_in[h], 16)
                if edge_attr is not None and whole:
                    sp.dma_start(attr[:, h, :, :].rearrange("p j f -> p (j f)"),
                                 edge_attr[at, :].rearrange("(p j) f -> p (j f)", j=J)).then_inc(attr_in[h], 16)

            load(0, 0, True)
            load(0, 1, True)
            with sp.Fori(1, NG // 2 - 1) as i:
                load(i, 0, False)
                load(i, 1, False)
            for h in range(2):
                g = NG - 2 + h
                load(NG // 2 - 1, h, False, whole=g < FULL)
                if edge_attr is not None and g == FULL:
                    tail = edge_attr[g * GE:g * GE + TAILP * J, :].rearrange("(p j) f -> p (j f)", j=J)
                    sp.dma_start(attr[0:TAILP, h, :, :].rearrange("p j f -> p (j f)"), tail).then_inc(attr_in[h], 16)
                    last = edge_attr[g * GE + TAILP * J:E, :].rearrange("(p j) f -> p (j f)", p=1)
                    sp.dma_start(attr[TAILP:TAILP + 1, h, 0:TAILJ, :].rearrange("p j f -> p (j f)"), last).then_inc(tail_in, 16)

        @block.gpsimd
        def _(pool):
            nc.gpsimd.iota(tri_i[:], pattern=[[1, P]], base=0, channel_multiplier=-1).then_inc(consts, 1)
            nc.gpsimd.iota(spare_i[:], pattern=[[0, J]], base=SPARE, channel_multiplier=1).then_inc(consts, 1)

            def gather(i, h, j, first):
                g = 2 * i + h
                if j == 0:
                    pool.wait_ge(at_in[h], 16 * (i + 1))
                    if not first:
                        pool.wait_ge(summed, J * (g - 1))
                    pool.sem_inc(turns, 1)
                nc.gpsimd.indirect_dma_start(
                    out=rows[:, h, j, :], out_offset=None, in_=rows_from,
                    in_offset=bass.IndirectOffsetOnAxis(ap=at_i[:, h, j:j + 1], axis=0)).then_inc(rows_in[h][j], 16)

            def scatter(i, h, j, first):
                g = 2 * i + h
                if j == 0:
                    pool.wait_ge(to_ready, g + 1)
                pool.wait_ge(staged, J * g + j + 1)
                if not (first and h == 0 and j < K):
                    pool.wait_ge(added[j % K], 16 * (per_table * g + j // K))
                pool.sem_inc(turns, 1)
                nc.gpsimd.indirect_dma_start(
                    out=tables[j % K], out_offset=bass.IndirectOffsetOnAxis(ap=to_i[:, h, j:j + 1], axis=0),
                    in_=sums[:, h, j, :], in_offset=None, compute_op=ALU.add).then_inc(added[j % K], 16)

            for j in range(J):
                gather(0, 0, j, True)
            for j in range(J):
                gather(0, 1, j, True)
                scatter(0, 0, j, True)
            with pool.Fori(1, NG // 2) as i:
                for j in range(J):
                    gather(i, 0, j, False)
                    scatter(i - 1, 1, j, False)
                for j in range(J):
                    gather(i, 1, j, False)
                    scatter(i, 0, j, False)
            for j in range(J):
                scatter(NG // 2 - 1, 1, j, False)
            for k in range(K):
                pool.wait_ge(added[k], 16 * per_table * NG)

        @block.vector
        def _(dve):
            dve.wait_ge(consts, 2)
            nc.vector.memset(one[:], 1.0).then_inc(ready, 1)
            nc.vector.tensor_copy(spare[:], spare_i[:]).then_inc(ready, 1)
            nc.vector.tensor_scalar(lower[:], tri_i[:], 0.0, None, ALU.is_lt).then_inc(ready, 1)
            dve.wait_ge(ready, 3)

            def half(i, h, first):
                g = 2 * i + h
                dve.wait_ge(key_in[h], 16 * keys_dmas * (i + 1))
                if not first:
                    dve.wait_ge(summed, J * (g - 1))
                for j in range(J):
                    nc.vector.scalar_tensor_tensor(junk[:, h, j, :], key_b[:, h, :, j], key_p[:, h, j:j + 1], lower[:],
                                                   ALU.is_equal, ALU.mult, accum_out=before[:, h, j:j + 1])
                    if weight is not None:
                        last = nc.vector.tensor_scalar(same[:, h, j, :], key_b[:, h, :, j], key_p[:, h, j:j + 1], w_p[:, h, j:j + 1],
                                                       ALU.is_equal, ALU.mult)
                    else:
                        last = nc.vector.tensor_scalar(same[:, h, j, :], key_b[:, h, :, j], key_p[:, h, j:j + 1], None, ALU.is_equal)
                    last.then_inc(same_ready, 1)
                dve.wait_ge(same_ready, J * (g + 1))
                nc.vector.tensor_scalar(before[:, h, :], before[:, h, :], 0.0, None, ALU.is_gt)
                nc.vector.tensor_tensor(to_f[:, h, :], spare[:], key_p[:, h, :], ALU.subtract).then_inc(step, 1)
                dve.wait_ge(step, 3 * g + 1)
                nc.vector.tensor_tensor(to_f[:, h, :], to_f[:, h, :], before[:, h, :], ALU.mult).then_inc(step, 1)
                dve.wait_ge(step, 3 * g + 2)
                nc.vector.tensor_tensor(to_f[:, h, :], to_f[:, h, :], key_p[:, h, :], ALU.add).then_inc(step, 1)
                dve.wait_ge(step, 3 * g + 3)
                if not first:
                    for k in range(K):
                        dve.wait_ge(added[k], 16 * per_table * (g - 1))
                nc.vector.tensor_copy(to_i[:, h, :], to_f[:, h, :]).then_inc(to_ready, 1)

            loop(dve, half)

        @block.tensor
        def _(pe):
            def half(i, h, first):
                g = 2 * i + h
                if edge_attr is not None:
                    pe.wait_ge(ready, 3)
                    pe.wait_ge(attr_in[h], 16 * (i + 1))
                    if isinstance(i, int) and 2 * i + h == FULL:
                        pe.wait_ge(tail_in, 16)
                for j in range(J):
                    pe.wait_ge(same_ready, J * g + j + 1)
                    pe.wait_ge(rows_in[h][j], 16 * (i + 1))
                    if not (first and h == 0 and j < K):
                        pe.wait_ge(staged, J * g + j + 1 - K)
                    last = nc.tensor.matmul(bank[j % K][:, 0:F], same[:, h, j, :], rows[:, h, j, :], start=True, stop=True)
                    if edge_attr is not None:
                        nc.tensor.matmul(bank[j % K][:, F:2 * F], same[:, h, j, :], attr[:, h, j, :], start=True, stop=True)
                        last = nc.tensor.matmul(bank[j % K][:, 2 * F:2 * F + 1], same[:, h, j, :], one[:], start=True, stop=True)
                    last.then_inc(summed, 1)

            loop(pe, half)

        @block.scalar
        def _(act):
            def half(i, h, first):
                g = 2 * i + h
                for j in range(J):
                    act.wait_ge(summed, J * g + j + 1)
                    if not first:
                        act.wait_ge(added[j % K], 16 * (per_table * (g - 2) + j // K + 1))
                    nc.scalar.copy(sums[:, h, j, :], bank[j % K][:, 0:width]).then_inc(staged, 1)

            loop(act, half)


def gcn_nodes(nc, d):
    with ExitStack() as ctx:
        sb = lambda name, shape, dt=F32: ctx.enter_context(nc.sbuf_tensor("n1_" + name, shape, dt))
        sem = semaphores(nc, ctx, "n1_")
        acc = sb("acc", [NP, NT, F])
        part = sb("part", [NP, 2, NT, F])
        x = sb("x", [NP, NT, F])
        tile = sb("tile", [NP, 2, F])
        accT = sb("accT", [F, 2, NP])
        w = sb("w", [F, F])
        bias = sb("bias", [NP, F])
        stat = sb("stat", [NP, 3, NT])
        turned = d.bank[0:2]
        prod = d.bank[2:4]
        acc_in, x_in, w_in = sem("acc_in"), sem("x_in"), sem("w_in")
        part_in = [sem(f"part_in{b}") for b in range(2)]
        part_used = sem("part_used")
        done = sem("done")
        agg_ready = sem("agg_ready")
        turn_ready = sem("turn_ready")
        accT_ready = sem("accT_ready")
        prod_ready = sem("prod_ready")
        prod_used = sem("prod_used")
        x1_part = sem("x1_part")
        x1_ready = sem("x1_ready")
        var_ready = sem("var_ready")
        std_ready = sem("std_ready")
        h_ready = sem("h_ready")
        stored = sem("stored")
        block = ctx.enter_context(nc.Block())
        nodes = lambda t: t[0:N, :].rearrange("(p t) f -> p t f", p=NP)

        @block.sync
        def _(sp):
            sp.dma_start(acc[:], nodes(d.g)).then_inc(acc_in, 16)
            for k, t in enumerate(d.tab0):
                if k >= 2:
                    sp.wait_ge(part_used, k - 1)
                sp.dma_start(part[:, k % 2, :, :], nodes(t)).then_inc(part_in[k % 2], 16)
            sp.dma_start(w[:], d.kernel).then_inc(w_in, 16)
            sp.dma_start(bias[:], d.bias.rearrange("(o f) -> o f", o=1).to_broadcast([NP, F])).then_inc(w_in, 16)
            sp.dma_start(x[:], nodes(d.x)).then_inc(x_in, 16)
            sp.wait_ge(x1_ready, 1)
            sp.dma_start(nodes(d.x1), x[:]).then_inc(stored, 16)
            sp.wait_ge(h_ready, 1)
            sp.dma_start(nodes(d.h1), acc[:]).then_inc(stored, 16)
            sp.wait_ge(stored, 32)

        @block.vector
        def _(dve):
            count = [0]

            def link(ins):
                count[0] += 1
                ins.then_inc(done, 1)
                dve.wait_ge(done, count[0])

            dve.wait_ge(acc_in, 16)
            for k in range(K):
                dve.wait_ge(part_in[k % 2], 16 * (k // 2 + 1))
                nc.vector.tensor_tensor(acc[:], acc[:], part[:, k % 2, :, :], ALU.add).then_inc(part_used, 1)
                dve.wait_ge(part_used, k + 1)
            dve.wait_ge(w_in, 32)
            dve.wait_ge(x_in, 16)
            with dve.Fori(0, NT // 2) as i:
                for b in range(2):
                    t = 2 * i + b
                    nc.vector.tensor_scalar(tile[:, b, :], acc[:, bass.ds(t, 1), :].rearrange("p a f -> p (a f)"),
                                            d.dinv[:, bass.ds(t, 1)], None, ALU.mult).then_inc(agg_ready, 1)
                    dve.wait_ge(prod_ready, t + 1)
                    nc.vector.tensor_tensor(part[:, b, 0, :], prod[b][0:NP, 0:F], bias[:], ALU.add).then_inc(prod_used, 1)
                    dve.wait_ge(prod_used, t + 1)
                    last = nc.vector.scalar_tensor_tensor(x[:, bass.ds(t, 1), :].rearrange("p a f -> p (a f)"), part[:, b, 0, :], 0.0,
                                                          x[:, bass.ds(t, 1), :].rearrange("p a f -> p (a f)"), ALU.max, ALU.add)
                    last.then_inc(x1_part, 1)
            dve.wait_ge(x1_part, NT)
            link(nc.vector.reduce_sum(stat[:, 0, :], x[:], AX_X))
            nc.vector.tensor_scalar(stat[:, 0, :], stat[:, 0, :], 1.0 / F, None, ALU.mult).then_inc(x1_ready, 1)
            dve.wait_ge(x1_ready, 1)
            link(nc.vector.tensor_tensor(acc[:], x[:], stat[:, 0, :].unsqueeze(2).to_broadcast([NP, NT, F]), ALU.subtract))
            link(nc.vector.tensor_tensor(part[:, 0, :, :], acc[:], acc[:], ALU.mult))
            link(nc.vector.reduce_sum(stat[:, 1, :], part[:, 0, :, :], AX_X))
            nc.vector.tensor_scalar(stat[:, 1, :], stat[:, 1, :], 1.0 / F, LN_EPS, ALU.mult, ALU.add).then_inc(var_ready, 1)
            dve.wait_ge(std_ready, 1)
            link(nc.vector.reciprocal(stat[:, 0, :], stat[:, 2, :]))
            link(nc.vector.tensor_tensor(acc[:], acc[:], stat[:, 0, :].unsqueeze(2).to_broadcast([NP, NT, F]), ALU.mult))
            nc.vector.tensor_scalar(acc[:], acc[:], 0.0, None, ALU.max).then_inc(h_ready, 1)

        @block.tensor
        def _(pe):
            pe.wait_ge(w_in, 32)
            with pe.Fori(0, NT // 2) as i:
                for b in range(2):
                    t = 2 * i + b
                    pe.wait_ge(agg_ready, t + 1)
                    nc.tensor.transpose(turned[b][:, 0:NP], tile[:, b, :], d.ident[0:NP, 0:NP]).then_inc(turn_ready, 1)
                    pe.wait_ge(accT_ready, t + 1)
                    nc.tensor.matmul(prod[b][0:NP, 0:F], accT[:, b, :], w[:], start=True, stop=True).then_inc(prod_ready, 1)
                    pe.wait_ge(prod_used, t + 1)

        @block.scalar
        def _(act):
            with act.Fori(0, NT // 2) as i:
                for b in range(2):
                    t = 2 * i + b
                    act.wait_ge(turn_ready, t + 1)
                    nc.scalar.copy(accT[:, b, :], turned[b][:, 0:NP]).then_inc(accT_ready, 1)
            act.wait_ge(var_ready, 1)
            nc.scalar.activation(stat[:, 2, :], stat[:, 1, :], ACT.Sqrt).then_inc(std_ready, 1)


def relational_sums(nc, d, name, tables, w_node, w_attr, bias, first):
    width = tables[0].shape[1]
    with ExitStack() as ctx:
        sb = lambda nm, shape, dt=F32: ctx.enter_context(nc.sbuf_tensor(f"{name}_{nm}", shape, dt))
        sem = semaphores(nc, ctx, name + "_")
        HT = NT // 2
        acc = sb("acc", [NP, HT, width])
        part = sb("part", [NP, 2, HT, width])
        turn_sb = sb("turn_sb", [F, 2, 2, NP])
        w = sb("w", [F, 2, F])
        b_sb = sb("b", [NP, F])
        turned = d.bank[0:2]
        prod = d.bank[2:4]
        w_in, acc_in = sem("w_in"), sem("acc_in")
        part_in = [sem(f"part_in{b}") for b in range(2)]
        part_used = sem("part_used")
        acc_ready = sem("acc_ready")
        acc_used = sem("acc_used")
        turn_ready, turn_copied = sem("turn_ready"), sem("turn_copied")
        prod_ready, prod_used = sem("prod_ready"), sem("prod_used")
        step = sem("step")
        scratch = sb("scratch", [NP, 2, F])

        def product_at(t):
            return d.agg[:, t, :] if first else scratch[:, t % 2, :]

        block = ctx.enter_context(nc.Block())

        def cols(t, r):
            return t[0:N, :].rearrange("(p t) f -> p t f", p=NP)[:, r * HT:(r + 1) * HT, :]

        @block.sync
        def _(sp):
            sp.dma_start(w[:, 0, :], w_node).then_inc(w_in, 16)
            sp.dma_start(w[:, 1, :], w_attr).then_inc(w_in, 16)
            sp.dma_start(b_sb[:], bias.rearrange("(o f) -> o f", o=1).to_broadcast([NP, F])).then_inc(w_in, 16)
            for r in range(2):
                if r:
                    sp.wait_ge(acc_used, HT)
                sp.dma_start(acc[:], cols(tables[0], r)).then_inc(acc_in, 16)
                for k in range(1, K):
                    n = r * (K - 1) + k - 1
                    if n >= 2:
                        sp.wait_ge(part_used, n - 1)
                    sp.dma_start(part[:, n % 2, :, :], cols(tables[k], r)).then_inc(part_in[n % 2], 16)

        @block.vector
        def _(dve):
            dve.wait_ge(w_in, 48)
            for r in range(2):
                dve.wait_ge(acc_in, 16 * (r + 1))
                for k in range(1, K):
                    n = r * (K - 1) + k - 1
                    dve.wait_ge(part_in[n % 2], 16 * (n // 2 + 1))
                    nc.vector.tensor_tensor(acc[:], acc[:], part[:, n % 2, :, :], ALU.add).then_inc(part_used, 1)
                    dve.wait_ge(part_used, n + 1)
                cnt = d.cnt[:, r * HT:(r + 1) * HT]
                here = acc[:, :, 2 * F]
                if first:
                    nc.vector.tensor_copy(cnt, here).then_inc(acc_ready, 1)
                else:
                    nc.vector.tensor_tensor(cnt, cnt, here, ALU.add).then_inc(acc_ready, 1)
                for tt in range(HT):
                    t = r * HT + tt
                    dve.wait_ge(prod_ready, t + 1)
                    nc.vector.scalar_tensor_tensor(product_at(t), b_sb[:], acc[:, tt, 2 * F:2 * F + 1], prod[t % 2][0:NP, 0:F],
                                                   ALU.mult, ALU.add).then_inc(prod_used, 1)
                    if not first:
                        dve.wait_ge(prod_used, t + 1)
                        nc.vector.tensor_tensor(d.agg[:, t, :], d.agg[:, t, :], product_at(t), ALU.add).then_inc(step, 1)

        @block.tensor
        def _(pe):
            pe.wait_ge(w_in, 48)
            for t in range(NT):
                r, tt = divmod(t, HT)
                if tt == 0:
                    pe.wait_ge(acc_ready, r + 1)
                for m in range(2):
                    if t >= 2:
                        pe.wait_ge(turn_copied, 2 * (t - 2) + m + 1)
                    last = nc.tensor.transpose(turned[m][:, (t % 2) * P:(t % 2) * P + NP], acc[:, tt, m * F:(m + 1) * F], d.ident[0:NP, 0:NP])
                    last.then_inc(turn_ready, 1)
                pe.wait_ge(turn_copied, 2 * t + 2)
                if t >= 2:
                    pe.wait_ge(prod_used, t - 1)
                for m in range(2):
                    last = nc.tensor.matmul(prod[t % 2][0:NP, 0:F], turn_sb[:, t % 2, m, :], w[:, m, :], start=(m == 0), stop=(m == 1))
                last.then_inc(prod_ready, 1)

        @block.scalar
        def _(act):
            for t in range(NT):
                for m in range(2):
                    act.wait_ge(turn_ready, 2 * t + m + 1)
                    if t >= 2:
                        act.wait_ge(prod_ready, t - 1)
                    nc.scalar.copy(turn_sb[:, t % 2, m, :], turned[m][:, (t % 2) * P:(t % 2) * P + NP]).then_inc(turn_copied, 1)
                if (t + 1) % HT == 0:
                    act.wait_ge(prod_used, t + 1)
                    act.sem_inc(acc_used, HT)


def last_nodes(nc, d):
    with ExitStack() as ctx:
        sb = lambda name, shape, dt=F32: ctx.enter_context(nc.sbuf_tensor("n2_" + name, shape, dt))
        sem = semaphores(nc, ctx, "n2_")
        h1 = sb("h1", [NP, NT, F])
        x1 = sb("x1", [NP, NT, F])
        work = sb("work", [NP, NT, F])
        gamma = sb("gamma", [NP, F])
        beta = sb("beta", [NP, F])
        stat = sb("stat", [NP, 3, NT])
        loaded, done = sem("loaded"), sem("done")
        var_ready, std_ready = sem("var_ready"), sem("std_ready")
        out_ready, stored = sem("out_ready"), sem("stored")
        block = ctx.enter_context(nc.Block())
        nodes = lambda t: t[0:N, :].rearrange("(p t) f -> p t f", p=NP)

        @block.sync
        def _(sp):
            sp.dma_start(h1[:], nodes(d.h1)).then_inc(loaded, 16)
            sp.dma_start(x1[:], nodes(d.x1)).then_inc(loaded, 16)
            for a, t in ((d.gamma, gamma), (d.beta, beta)):
                sp.dma_start(t[:], a.rearrange("(o f) -> o f", o=1).to_broadcast([NP, F])).then_inc(loaded, 16)
            sp.wait_ge(out_ready, 1)
            sp.dma_start(nodes(d.out), work[:]).then_inc(stored, 16)
            sp.wait_ge(stored, 16)

        @block.scalar
        def _(act):
            act.wait_ge(var_ready, 1)
            nc.scalar.activation(stat[:, 2, :], stat[:, 1, :], ACT.Sqrt).then_inc(std_ready, 1)

        @block.vector
        def _(dve):
            count = [0]

            def link(ins):
                count[0] += 1
                ins.then_inc(done, 1)
                dve.wait_ge(done, count[0])

            per_node = lambda r: stat[:, r, :].unsqueeze(2).to_broadcast([NP, NT, F])
            per_feature = lambda a: a[:].unsqueeze(1).to_broadcast([NP, NT, F])
            agg = d.agg
            link(nc.vector.tensor_scalar(stat[:, 0, :], d.cnt[:], AGG_EPS, None, ALU.add))
            link(nc.vector.reciprocal(stat[:, 1, :], stat[:, 0, :]))
            link(nc.vector.tensor_tensor(agg[:], agg[:], per_node(1), ALU.mult))
            link(nc.vector.scalar_tensor_tensor(agg[:], agg[:], SLOPE, agg[:], ALU.mult, ALU.max))
            dve.wait_ge(loaded, 64)
            link(nc.vector.tensor_tensor(agg[:], agg[:], h1[:], ALU.add))
            link(nc.vector.reduce_sum(stat[:, 0, :], agg[:], AX_X))
            link(nc.vector.tensor_scalar(stat[:, 0, :], stat[:, 0, :], 1.0 / F, None, ALU.mult))
            link(nc.vector.tensor_tensor(agg[:], agg[:], per_node(0), ALU.subtract))
            link(nc.vector.tensor_tensor(work[:], agg[:], agg[:], ALU.mult))
            link(nc.vector.reduce_sum(stat[:, 1, :], work[:], AX_X))
            nc.vector.tensor_scalar(stat[:, 1, :], stat[:, 1, :], 1.0 / F, LN_EPS, ALU.mult, ALU.add).then_inc(var_ready, 1)
            dve.wait_ge(std_ready, 1)
            link(nc.vector.reciprocal(stat[:, 0, :], stat[:, 2, :]))
            link(nc.vector.tensor_tensor(agg[:], agg[:], per_feature(gamma), ALU.mult))
            link(nc.vector.tensor_tensor(agg[:], agg[:], per_node(0), ALU.mult))
            link(nc.vector.tensor_tensor(agg[:], agg[:], per_feature(beta), ALU.add))
            nc.vector.tensor_tensor(work[:], agg[:], x1[:], ALU.add).then_inc(out_ready, 1)


def constants(nc, d):
    with ExitStack() as ctx:
        zero = ctx.enter_context(nc.sbuf_tensor("pad_rows", [(ROWS - N) // 2, 2 * F], F32))
        sem = semaphores(nc, ctx, "const_")
        zeroed, ident_ready, stored = sem("zeroed"), sem("ident_ready"), sem("stored")
        block = ctx.enter_context(nc.Block())

        @block.gpsimd
        def _(pool):
            nc.gpsimd.memset(d.ident[:], 0.0).then_inc(ident_ready, 1)
            pool.wait_ge(ident_ready, 1)
            nc.gpsimd.affine_select(out=d.ident[:], in_=d.ident[:], compare_op=ALU.not_equal, fill=1.0, base=0,
                                    pattern=[[-1, P]], channel_multiplier=1).then_inc(ident_ready, 1)
            pool.wait_ge(ident_ready, 2)

        @block.vector
        def _(dve):
            nc.vector.memset(zero[:], 0.0).then_inc(zeroed, 1)

        @block.sync
        def _(sp):
            sp.wait_ge(zeroed, 1)
            for t in (d.g, d.h1):
                sp.dma_start(t[N:ROWS, :].rearrange("(p r) f -> p (r f)", r=2), zero[:]).then_inc(stored, 16)
            sp.wait_ge(stored, 32)


def program(nc, d):
    dram = lambda name, shape, dt=F32: nc.dram_tensor(name, shape, dt).ap()
    d.src_i, d.dst_i = dram("src_pad", (EP,), I32), dram("dst_pad", (EP,), I32)
    d.src_f, d.dst_f, d.wp = dram("src_key", (EP,)), dram("dst_key", (EP,)), dram("w_pad", (EP,))
    d.g, d.h1, d.x1 = dram("g", (ROWS, F)), dram("h1", (ROWS, F)), dram("x1", (ROWS, F))
    d.tab0 = [dram(f"gcn_sums{k}", (ROWS, F)) for k in range(K)]
    d.tab_f = [dram(f"fwd_sums{k}", (ROWS, 2 * F + 1)) for k in range(K)]
    d.tab_b = [dram(f"back_sums{k}", (ROWS, 2 * F + 1)) for k in range(K)]
    with ExitStack() as ctx:
        d.dinv = ctx.enter_context(nc.sbuf_tensor("dinv", [NP, NT], F32))
        d.cnt = ctx.enter_context(nc.sbuf_tensor("cnt", [NP, NT], F32))
        d.ident = ctx.enter_context(nc.sbuf_tensor("ident", [P, P], F32))
        d.bank = [ctx.enter_context(nc.psum_tensor(f"bank{b}", [P, 512], F32)) for b in range(8)]
        constants(nc, d)
        clear_tables(nc, d.tab0 + d.tab_f + d.tab_b)
        setup_and_degrees(nc, d)
        edge_pass(nc, d, "gcn", d.g, d.dst_i, d.src_f, d.wp, None, d.tab0)
        gcn_nodes(nc, d)
        edge_pass(nc, d, "fwd", d.h1, d.src_i, d.dst_f, None, d.edge_attr, d.tab_f)
        edge_pass(nc, d, "back", d.h1, d.dst_i, d.src_f, None, d.edge_attr, d.tab_b)
        with nc.sbuf_tensor("agg", [NP, NT, F], F32) as d.agg:
            relational_sums(nc, d, "rf", d.tab_f, d.w_fwd[0:F, :], d.w_fwd[F:2 * F, :], d.b_fwd, True)
            relational_sums(nc, d, "rb", d.tab_b, d.w_back[0:F, :], d.w_back[F:2 * F, :], d.b_back, False)
            last_nodes(nc, d)


INPUTS = {"x": "x", "src": "src", "dst": "dst", "edge_attr_128": "edge_attr", "edge_weight": "w", "L0_gnn_kernel": "kernel",
          "L0_gnn_bias": "bias", "L1_gnn_W_fwd": "w_fwd", "L1_gnn_b_fwd": "b_fwd", "L1_gnn_W_back": "w_back",
          "L1_gnn_b_back": "b_back", "L1_gnn_gamma": "gamma", "L1_gnn_beta": "beta"}


def kernel(**inputs):
    import concourse.bacc as bacc
    from concourse.bass_utils import run_bass_kernel_spmd as run

    nc = bacc.Bacc("TRN2", target_bir_lowering=False, num_devices=1)
    d = Net()
    arrays = {}
    for name, short in INPUTS.items():
        a = np.ascontiguousarray(inputs[name])
        arrays[f"in_{name}"] = a
        d.__dict__[short] = nc.dram_tensor(f"in_{name}", a.shape, mybir.dt.from_np(a.dtype), kind="ExternalInput").ap()
    d.out = nc.dram_tensor("out", (N, F), F32, kind="ExternalOutput").ap()
    program(nc, d)
    return run(nc, [arrays], core_ids=[0]).results[0]["out"]
```

```python
from contextlib import ExitStack

import numpy as np
import concourse.bass as bass
from concourse import mybir

F32 = mybir.dt.float32
I32 = mybir.dt.int32
ALU = mybir.AluOpType
ACT = mybir.ActivationFunctionType
AX_X = mybir.AxisListType.X

N = 6250
E = 206250
F = 128
P = 128
NP, NT = 125, 50
J = 8
GE = P * J
NG = 2 * -(-E // (2 * GE))
EP = NG * GE
FULL = E // GE
TAILP, TAILJ = divmod(E - FULL * GE, J)
PADKEY = N
SPARE = N + 1
ROWS = 6400
REC = 4
K = 4
LN_EPS = 1e-5
AGG_EPS = 1e-7
SLOPE = 0.01
ROUND = 12582912.0


def semaphores(nc, ctx, prefix):
    taken = []

    def sem(name):
        taken.append(nc.alloc_semaphore(prefix + name))
        return taken[-1]

    def clear():
        nc.clear_and_free_semaphores(taken)
        nc.all_engine_barrier()

    ctx.callback(clear)
    return sem


class Net:
    pass


def setup_and_degrees(nc, d):
    with ExitStack() as ctx:
        sb = lambda name, shape, dt=F32: ctx.enter_context(nc.sbuf_tensor(name, shape, dt))
        sem = semaphores(nc, ctx, "setup_")
        widest = max(t.shape[1] for t in d.cleared)
        zeros = sb("zeros", [P, ROWS // P // 5 * widest])
        src_i = sb("src_i", [P, NG, J], I32)
        dst_i = sb("dst_i", [P, NG, J], I32)
        rec = sb("rec", [P, NG, REC, J])
        row_of = sb("row_of", [P, NG, J])
        col_of = sb("col_of", [P, NG, J])
        base_b = sb("base_b", [P, NG])
        wide = sb("wide", [P, 4])
        iota_i = sb("iota_i", [P, P], I32)
        row_hot = sb("row_hot", [P, 2, J, NP])
        col_hot = sb("col_hot", [P, 2, J, NT])
        col_any = sb("col_any", [P, 2, J, NT])
        deg = sb("deg", [NP, NT])
        has_edge = sb("has_edge", [NP, NT])
        x = sb("x_sb", [NP, NT, F])
        xc = sb("xc", [NP, NT, F])
        stat = sb("stat", [NP, 3, NT])
        src_f, dst_f, rel_f, w = (rec[:, :, r, :] for r in range(REC))
        hist, spread = d.bank[0:2], d.bank[2]
        edges_in = sem("edges_in")
        x_in = sem("x_in")
        zeroed = sem("zeroed")
        pads = sem("pads")
        iota_ready = sem("iota_ready")
        ident_ready = sem("ident_ready")
        done = sem("done")
        dst_ready = sem("dst_ready")
        base_ready = sem("base_ready")
        wide_ready = sem("wide_ready")
        wide_summed = sem("wide_summed")
        rec_ready = sem("rec_ready")
        var_ready = sem("var_ready")
        std_ready = sem("std_ready")
        g_ready = sem("g_ready")
        hot_ready = sem("hot_ready")
        hist_ready = sem("hist_ready")
        hist_used = sem("hist_used")
        step = sem("step")
        stored = sem("stored")
        cleared = sem("cleared")
        block = ctx.enter_context(nc.Block())

        @block.sync
        def _(sp):
            sp.dma_start(x[:], d.x.rearrange("(p t) f -> p t f", p=NP)).then_inc(x_in, 16)
            sp.wait_ge(pads, 3)
            for a, t in ((d.src, src_i[:]), (d.dst, dst_i[:]), (d.w, w)):
                sp.dma_start(t[:, 0:FULL, :], a[0:FULL * GE].rearrange("(g p j) -> p g j", p=P, j=J)).then_inc(edges_in, 16)
                at = FULL * GE
                sp.dma_start(t[0:TAILP, FULL, :], a[at:at + TAILP * J].rearrange("(p j) -> p j", j=J)).then_inc(edges_in, 16)
                sp.dma_start(t[TAILP:TAILP + 1, FULL, 0:TAILJ], a[at + TAILP * J:E].rearrange("(p j) -> p j", p=1)).then_inc(edges_in, 16)
            sp.wait_ge(rec_ready, 1)
            linear = lambda a: a.rearrange("(g p j) -> p g j", p=P, j=J)
            for a, t in ((d.src_i, src_i[:]), (d.dst_i, dst_i[:]), (d.src_f, src_f), (d.dst_f, dst_f), (d.rel_f, rel_f)):
                sp.dma_start(linear(a), t).then_inc(stored, 16)
            sp.dma_start(d.rec.rearrange("g p r -> p g r"), rec[:].rearrange("p g r j -> p g (r j)")).then_inc(stored, 16)
            sp.wait_ge(zeroed, 1)
            for t in d.cleared:
                c = t.shape[1]
                view = t.rearrange("(p q r) c -> p q (r c)", p=P, q=5)
                for q in range(5):
                    sp.dma_start(view[:, q, :], zeros[:, 0:ROWS // P // 5 * c]).then_inc(cleared, 16)
            for t in (d.g, d.h1):
                sp.dma_start(t[N:ROWS, :].rearrange("(p r) f -> p (r f)", r=2), zeros[0:(ROWS - N) // 2, 0:2 * F]).then_inc(cleared, 16)
            sp.wait_ge(g_ready, 1)
            sp.dma_start(d.g[0:N, :].rearrange("(p t) f -> p t f", p=NP), xc[:]).then_inc(stored, 16)
            sp.wait_ge(stored, 16 * 7)
            sp.wait_ge(cleared, 16 * (5 * len(d.cleared) + 2))

        @block.gpsimd
        def _(pool):
            nc.gpsimd.memset(d.ident[:], 0.0).then_inc(ident_ready, 1)
            nc.gpsimd.memset(d.ones[:], 1.0).then_inc(iota_ready, 1)
            nc.gpsimd.iota(iota_i[:], pattern=[[1, P]], base=0, channel_multiplier=0).then_inc(iota_ready, 1)
            nc.gpsimd.iota(d.part_i[:], pattern=[[0, J]], base=0, channel_multiplier=1).then_inc(iota_ready, 1)
            pool.wait_ge(ident_ready, 1)
            nc.gpsimd.affine_select(out=d.ident[:], in_=d.ident[:], compare_op=ALU.not_equal, fill=1.0, base=0,
                                    pattern=[[-1, P]], channel_multiplier=1).then_inc(ident_ready, 1)
            pool.wait_ge(ident_ready, 2)
            for t in (d.attr_sums, d.row_sums, d.row_count):
                nc.gpsimd.memset(t[:], 0.0).then_inc(ident_ready, 1)
            nc.gpsimd.memset(zeros[:], 0.0).then_inc(zeroed, 1)

        @block.scalar
        def _(act):
            act.wait_ge(var_ready, 1)
            nc.scalar.activation(stat[:, 2, :], stat[:, 1, :], ACT.Sqrt).then_inc(std_ready, 1)
            act.wait_ge(var_ready, 2)
            nc.scalar.activation(stat[:, 2, :], deg[:], ACT.Sqrt).then_inc(std_ready, 1)

        @block.vector
        def _(dve):
            count = [0]

            def link(ins):
                count[0] += 1
                ins.then_inc(done, 1)
                dve.wait_ge(done, count[0])

            nc.vector.memset(src_i[:, FULL:, :], PADKEY).then_inc(pads, 1)
            nc.vector.memset(dst_i[:, FULL:, :], PADKEY).then_inc(pads, 1)
            nc.vector.memset(w[:, FULL:, :], 0.0).then_inc(pads, 1)
            nc.vector.memset(deg[:], 1.0)
            dve.wait_ge(iota_ready, 3)
            nc.vector.tensor_copy(d.iota[:], iota_i[:])
            link(nc.vector.tensor_copy(d.part[:], d.part_i[:]))
            nc.vector.tensor_tensor(d.before_me[:], d.iota[:], d.part[:, 0:1].to_broadcast([P, P]), ALU.is_lt)
            link(nc.vector.tensor_scalar(d.spare[:], d.part[:], float(SPARE), None, ALU.add))
            dve.wait_ge(edges_in, 16 * 9)
            nc.vector.tensor_copy(src_f, src_i[:])
            nc.vector.tensor_copy(dst_f, dst_i[:]).then_inc(dst_ready, 1)
            dve.wait_ge(dst_ready, 1)
            link(nc.vector.tensor_scalar(row_of[:], src_f, 1.0 / NT, 0.5 / NT - 0.5, ALU.mult, ALU.add))
            link(nc.vector.tensor_scalar(row_of[:], row_of[:], ROUND, ROUND, ALU.add, ALU.subtract))
            link(nc.vector.scalar_tensor_tensor(col_of[:], row_of[:], -float(NT), src_f, ALU.mult, ALU.add))
            dve.wait_ge(base_ready, 1)
            link(nc.vector.tensor_copy(base_b[:], spread[:, 0:NG]))
            nc.vector.tensor_copy(d.base_i[:], base_b[0:1, :])
            nc.vector.tensor_tensor(rel_f, dst_f, base_b[:].unsqueeze(2).to_broadcast([P, NG, J]), ALU.subtract).then_inc(rec_ready, 1)
            dve.wait_ge(rec_ready, 1)
            nc.vector.tensor_reduce(wide[:, 0:1], rel_f, mybir.AxisListType.XY, ALU.max)
            link(nc.vector.tensor_reduce(wide[:, 1:2], rel_f, mybir.AxisListType.XY, ALU.min))
            nc.vector.tensor_scalar(wide[:, 0:1], wide[:, 0:1], P - 0.5, None, ALU.is_gt)
            link(nc.vector.tensor_scalar(wide[:, 1:2], wide[:, 1:2], -0.5, None, ALU.is_lt))
            nc.vector.tensor_tensor(wide[:, 2:3], wide[:, 0:1], wide[:, 1:2], ALU.max).then_inc(wide_ready, 1)

            dve.wait_ge(x_in, 16)
            link(nc.vector.reduce_sum(stat[:, 0, :], x[:], AX_X))
            link(nc.vector.tensor_scalar(stat[:, 0, :], stat[:, 0, :], 1.0 / F, None, ALU.mult))
            link(nc.vector.tensor_tensor(xc[:], x[:], stat[:, 0, :].unsqueeze(2).to_broadcast([NP, NT, F]), ALU.subtract))
            link(nc.vector.tensor_tensor(x[:], xc[:], xc[:], ALU.mult))
            link(nc.vector.reduce_sum(stat[:, 1, :], x[:], AX_X))
            nc.vector.tensor_scalar(stat[:, 1, :], stat[:, 1, :], 1.0 / F, LN_EPS, ALU.mult, ALU.add).then_inc(var_ready, 1)
            dve.wait_ge(std_ready, 1)
            link(nc.vector.reciprocal(stat[:, 0, :], stat[:, 2, :]))
            link(nc.vector.tensor_tensor(xc[:], xc[:], stat[:, 0, :].unsqueeze(2).to_broadcast([NP, NT, F]), ALU.mult))
            link(nc.vector.tensor_scalar(xc[:], xc[:], 0.0, None, ALU.max))
            dve.wait_ge(wide_summed, 1)
            nc.vector.tensor_scalar(d.windowed[:], spread[0:1, 256:257], 0.5, None, ALU.is_lt)

            def one_hots(g, h):
                at = bass.ds(g, 1)
                per_edge = lambda t, n: t[:, at, :].rearrange("p o j -> p (o j)").unsqueeze(2).to_broadcast([P, J, n])
                numbers = lambda n: d.iota[:, 0:n].unsqueeze(1).to_broadcast([P, J, n])
                nc.vector.tensor_tensor(col_any[:, h, :, :], numbers(NT), per_edge(col_of, NT), ALU.is_equal).then_inc(step, 1)
                nc.vector.tensor_tensor(row_hot[:, h, :, :], numbers(NP), per_edge(row_of, NP), ALU.is_equal)
                dve.wait_ge(step, g + 1)
                nc.vector.tensor_tensor(col_hot[:, h, :, :], col_any[:, h, :, :], per_edge(w, NT), ALU.mult).then_inc(hot_ready, 1)

            one_hots(0, 0)
            one_hots(1, 1)
            dve.wait_ge(hist_ready, 1)
            nc.vector.tensor_tensor(deg[:], deg[:], hist[0][0:NP, 0:NT], ALU.add).then_inc(hist_used, 1)
            with dve.Fori(1, NG // 2) as i:
                for h in range(2):
                    g = 2 * i + h
                    dve.wait_ge(hist_ready, g - 1)
                    one_hots(g, h)
                    dve.wait_ge(hist_ready, g)
                    dve.wait_ge(hist_used, g - 1)
                    nc.vector.tensor_tensor(deg[:], deg[:], hist[1 - h][0:NP, 0:NT], ALU.add).then_inc(hist_used, 1)
            dve.wait_ge(hist_ready, NG)
            dve.wait_ge(hist_used, NG - 1)
            link(nc.vector.tensor_tensor(deg[:], deg[:], hist[1][0:NP, 0:NT], ALU.add))

            link(nc.vector.tensor_scalar(has_edge[:], deg[:], 0.0, None, ALU.is_gt))
            nc.vector.tensor_scalar(deg[:], deg[:], 1e-30, None, ALU.max).then_inc(var_ready, 1)
            dve.wait_ge(std_ready, 2)
            link(nc.vector.reciprocal(stat[:, 0, :], stat[:, 2, :]))
            link(nc.vector.tensor_tensor(d.dinv[:], stat[:, 0, :], has_edge[:], ALU.mult))
            nc.vector.tensor_tensor(xc[:], xc[:], d.dinv[:].unsqueeze(2).to_broadcast([NP, NT, F]), ALU.mult).then_inc(g_ready, 1)

        @block.tensor
        def _(pe):
            pe.wait_ge(dst_ready, 1)
            pe.wait_ge(iota_ready, 3)
            nc.tensor.matmul(spread[:, 0:NG], d.ones[0:1, :], dst_f[0:1, :, 0], start=True, stop=True).then_inc(base_ready, 1)
            pe.wait_ge(wide_ready, 1)
            nc.tensor.matmul(spread[0:1, 256:257], wide[:, 2:3], d.ones[:, 0:1], start=True, stop=True).then_inc(wide_summed, 1)

            def half(i, h, first):
                g = 2 * i + h
                pe.wait_ge(hot_ready, g + 1)
                if not first:
                    pe.wait_ge(hist_used, g - 1)
                for j in range(J):
                    last = nc.tensor.matmul(hist[h][0:NP, 0:NT], row_hot[:, h, j, :], col_hot[:, h, j, :],
                                            start=(j == 0), stop=(j == J - 1))
                last.then_inc(hist_ready, 1)

            half(0, 0, True)
            half(0, 1, True)
            with pe.Fori(1, NG // 2) as i:
                half(i, 0, False)
                half(i, 1, False)


def edge_pass(nc, d, name, rows_from, row_at, key_row, tables, weighted=False, attr=False, window_sums=None, sums_rows_at=None):
    width = tables[0].shape[1]
    windowed = row_at is None
    gather_at = sums_rows_at if windowed else row_at
    key_lin = (d.src_f, d.dst_f)[key_row]
    with ExitStack() as ctx:
        sb = lambda nm, shape, dt=F32: ctx.enter_context(nc.sbuf_tensor(f"{name}_{nm}", shape, dt))
        sem = semaphores(nc, ctx, name + "_")
        rec = sb("rec", [P, 2, REC, J])
        key_b = sb("key_b", [P, 2, P, J])
        same = sb("same", [P, 2, J, P])
        earlier = sb("earlier", [P, J, P])
        before = sb("before", [P, J])
        to_f = sb("to_f", [P, J])
        to_i = sb("to_i", [P, 2, J], I32)
        pay = sb("pay", [P, 2, J, F])
        sums = sb("sums", [P, 2, J, width])
        if gather_at is not None:
            at_i = sb("at_i", [P, 2, J], I32)
            rows = sb("rows", [P, 2, J, F])
        if attr:
            attrs = sb("attrs", [P, 2, J, F])
        if windowed:
            rel_b = sb("rel_b", [P, 2, P, J])
            window = sb("window", [P, 2, F])
            spread_hot = sb("spread_hot", [P, 2, J, P])
            sum_hot = sb("sum_hot", [P, 2, J, P])
        B = 2 if window_sums == "rows" else 4
        bank, count_bank, row_bank, win_bank = d.bank[0:B], d.bank[2:4], d.bank[4:6], d.bank[6:8]
        rec_in = [sem(f"rec_in{h}") for h in range(2)]
        key_in = [sem(f"key_in{h}") for h in range(2)]
        at_in = [sem(f"at_in{h}") for h in range(2)]
        attr_in = [sem(f"attr_in{h}") for h in range(2)]
        tail_in = sem("tail_in")
        rel_in = [sem(f"rel_in{h}") for h in range(2)]
        window_in = [sem(f"window_in{h}") for h in range(2)]
        rows_in = [[sem(f"rows_in{h}_{j}") for j in range(J)] for h in range(2)] if gather_at is not None else None
        spread_ready, same_ready, sum_ready = sem("spread_ready"), sem("same_ready"), sem("sum_ready")
        step, to_ready = sem("step"), sem("to_ready")
        row_ready = sem("row_ready")
        paid = sem("paid")
        summed = sem("summed")
        group_done = sem("group_done")
        window_added = sem("window_added")
        staged = sem("staged")
        turns = sem("turns")
        added = [sem(f"added{k}") for k in range(K)]
        per_table = J // K
        LAST = NG // 2 - 1
        block = ctx.enter_context(nc.Block())

        def loop(eng, half):
            half(0, 0, True)
            half(0, 1, True)
            with eng.Fori(1, LAST) as i:
                half(i, 0, False)
                half(i, 1, False)
            half(LAST, 0, False)
            half(LAST, 1, False)

        def group_at(g):
            return slice(g * GE, (g + 1) * GE) if isinstance(g, int) else bass.ds(g * GE, GE)

        @block.sync
        def _(sp):
            def half(i, h, first):
                g = 2 * i + h
                if not first:
                    sp.wait_ge(group_done, g - 1)
                    sp.wait_ge(to_ready, g - 1)
                everywhere = lambda a: a[group_at(g)].rearrange("(o e) -> o e", o=1).to_broadcast([P, GE])
                flat = lambda t: t[:, h, :, :].rearrange("p q j -> p (q j)")
                sp.dma_start(rec[:, h, :, :].rearrange("p r j -> p (r j)"),
                             d.rec[bass.ds(g, 1), :, :].rearrange("o p r -> (o p) r")).then_inc(rec_in[h], 16)
                if windowed:
                    sp.dma_start(flat(rel_b), everywhere(d.rel_f)).then_inc(rel_in[h], 16)
                    base = sp.value_load(d.base_i[0:1, bass.ds(g, 1)], min_val=0, max_val=N)
                    sp.dma_start(window[:, h, :], rows_from[bass.ds(base, P), :]).then_inc(window_in[h], 16)
                sp.dma_start(flat(key_b), everywhere(key_lin)).then_inc(key_in[h], 16)
                if gather_at is not None:
                    sp.dma_start(at_i[:, h, :], gather_at[group_at(g)].rearrange("(p j) -> p j", j=J)).then_inc(at_in[h], 16)
                if attr and not (isinstance(g, int) and g == FULL):
                    sp.dma_start(flat(attrs), d.edge_attr[group_at(g), :].rearrange("(p j) f -> p (j f)", j=J)).then_inc(attr_in[h], 16)
                if attr and isinstance(g, int) and g == FULL:
                    at = g * GE + TAILP * J
                    sp.dma_start(flat(attrs[0:TAILP]), d.edge_attr[g * GE:at, :].rearrange("(p j) f -> p (j f)", j=J)).then_inc(attr_in[h], 16)
                    sp.dma_start(attrs[TAILP:TAILP + 1, h, 0:TAILJ, :].rearrange("p j f -> p (j f)"),
                                 d.edge_attr[at:E, :].rearrange("(p j) f -> p (j f)", p=1)).then_inc(tail_in, 16)

            loop(sp, half)

        @block.gpsimd
        def _(pool):
            def gather(i, h, j, first):
                g = 2 * i + h
                if gather_at is None:
                    return
                if j == 0:
                    pool.wait_ge(at_in[h], 16 * (i + 1))
                    if not first:
                        pool.wait_ge(group_done, g - 1)
                        if not windowed:
                            pool.wait_ge(paid, J * (g - 1))
                    pool.sem_inc(turns, 1)
                nc.gpsimd.indirect_dma_start(
                    out=rows[:, h, j, :], out_offset=None, in_=rows_from,
                    in_offset=bass.IndirectOffsetOnAxis(ap=at_i[:, h, j:j + 1], axis=0)).then_inc(rows_in[h][j], 16)

            def scatter(i, h, j, first):
                g = 2 * i + h
                if j == 0:
                    pool.wait_ge(to_ready, g + 1)
                pool.wait_ge(staged, J * g + j + 1)
                if not (first and h == 0 and j < K):
                    pool.wait_ge(added[j % K], 16 * (per_table * g + j // K))
                pool.sem_inc(turns, 1)
                nc.gpsimd.indirect_dma_start(
                    out=tables[j % K], out_offset=bass.IndirectOffsetOnAxis(ap=to_i[:, h, j:j + 1], axis=0),
                    in_=sums[:, h, j, :], in_offset=None, compute_op=ALU.add).then_inc(added[j % K], 16)

            for j in range(J):
                gather(0, 0, j, True)
            for j in range(J):
                gather(0, 1, j, True)
                scatter(0, 0, j, True)
            with pool.Fori(1, NG // 2) as i:
                for j in range(J):
                    gather(i, 0, j, False)
                    scatter(i - 1, 1, j, False)
                for j in range(J):
                    gather(i, 1, j, False)
                    scatter(i, 0, j, False)
            for j in range(J):
                scatter(LAST, 1, j, False)
            for k in range(K):
                pool.wait_ge(added[k], 16 * per_table * NG)

        @block.vector
        def _(dve):
            def add_window(g, h):
                dve.wait_ge(group_done, g + 1)
                base = dve.value_load(d.base_i[0:1, bass.ds(g, 1)], min_val=0, max_val=N)
                if not isinstance(g, int) or g > 0:
                    dve.wait_ge(window_added, g)
                at = bass.ds(base, P)
                if window_sums == "rows":
                    nc.vector.tensor_tensor(d.row_count[0:1, at], d.row_count[0:1, at], count_bank[h][0:1, 0:P], ALU.add)
                total = d.row_sums if window_sums == "rows" else d.attr_sums
                nc.vector.tensor_tensor(total[:, at], total[:, at], win_bank[h][:, 0:P], ALU.add).then_inc(window_added, 1)

            def half(i, h, first):
                g = 2 * i + h
                dve.wait_ge(rec_in[h], 16 * (i + 1))
                if not first:
                    dve.wait_ge(group_done, g - 1)
                per_edge = lambda r: rec[:, h, r, :].unsqueeze(2).to_broadcast([P, J, P])
                by_chunk = lambda t: t[:, h, :, :].rearrange("p q j -> p j q")
                if windowed:
                    dve.wait_ge(rel_in[h], 16 * (i + 1))
                    nc.vector.tensor_scalar(spread_hot[:, h, :, :], by_chunk(rel_b), d.part[:, 0:1], None, ALU.is_equal).then_inc(spread_ready, 1)
                dve.wait_ge(key_in[h], 16 * (i + 1))
                nc.vector.tensor_tensor(same[:, h, :, :], by_chunk(key_b), per_edge(key_row), ALU.is_equal).then_inc(same_ready, 1)
                if windowed:
                    nc.vector.tensor_tensor(sum_hot[:, h, :, :], d.iota[:].unsqueeze(1).to_broadcast([P, J, P]), per_edge(2),
                                            ALU.is_equal).then_inc(sum_ready, 1)
                dve.wait_ge(same_ready, g + 1)
                nc.vector.tensor_tensor(earlier[:], same[:, h, :, :], d.before_me[:].unsqueeze(1).to_broadcast([P, J, P]), ALU.mult).then_inc(step, 1)
                nc.vector.tensor_tensor(to_f[:], d.spare[:], rec[:, h, key_row, :], ALU.subtract)
                dve.wait_ge(step, 5 * g + 1)
                nc.vector.reduce_sum(before[:], earlier[:], AX_X).then_inc(step, 1)
                dve.wait_ge(step, 5 * g + 2)
                nc.vector.tensor_scalar(before[:], before[:], 0.0, None, ALU.is_gt).then_inc(step, 1)
                dve.wait_ge(step, 5 * g + 3)
                nc.vector.tensor_tensor(to_f[:], to_f[:], before[:], ALU.mult).then_inc(step, 1)
                dve.wait_ge(step, 5 * g + 4)
                nc.vector.tensor_tensor(to_f[:], to_f[:], rec[:, h, key_row, :], ALU.add).then_inc(step, 1)
                dve.wait_ge(step, 5 * g + 5)
                if not first:
                    for k in range(K):
                        dve.wait_ge(added[k], 16 * per_table * (g - 1))
                nc.vector.tensor_copy(to_i[:, h, :], to_f[:]).then_inc(to_ready, 1)
                dve.wait_ge(to_ready, g + 1)
                if windowed and not (first and h == 0):
                    add_window(g - 1, 1 - h)

            loop(dve, half)
            if windowed:
                add_window(NG - 1, 1)

        @block.tensor
        def _(pe):
            def half(i, h, first):
                g = 2 * i + h

                def spread(j):
                    if not windowed or j >= J:
                        return
                    if not (first and h == 0 and j < 2):
                        pe.wait_ge(paid, J * g + j - 1)
                    nc.tensor.matmul(row_bank[j % 2][:, 0:F], spread_hot[:, h, j, :], window[:, h, :], start=True, stop=True).then_inc(row_ready, 1)

                if windowed:
                    pe.wait_ge(spread_ready, g + 1)
                    pe.wait_ge(window_in[h], 16 * (i + 1))
                spread(0)
                spread(1)
                pe.wait_ge(same_ready, g + 1)
                if windowed:
                    pe.wait_ge(sum_ready, g + 1)
                    if not first:
                        pe.wait_ge(window_added, g - 1)
                if attr:
                    pe.wait_ge(attr_in[h], 16 * (i + 1))
                    if isinstance(i, int) and g == FULL:
                        pe.wait_ge(tail_in, 16)
                for j in range(J):
                    ends = dict(start=(j == 0), stop=(j == J - 1))
                    if window_sums == "attr":
                        nc.tensor.matmul(win_bank[h][:, 0:P], attrs[:, h, j, :], sum_hot[:, h, j, :], **ends)
                    if window_sums == "rows":
                        pe.wait_ge(rows_in[h][j], 16 * (i + 1))
                        nc.tensor.matmul(win_bank[h][:, 0:P], rows[:, h, j, :], sum_hot[:, h, j, :], **ends)
                        nc.tensor.matmul(count_bank[h][0:1, 0:P], d.ones[:, 0:1], sum_hot[:, h, j, :], **ends)
                    pe.wait_ge(paid, J * g + j + 1)
                    if not (first and h == 0 and j < B):
                        pe.wait_ge(staged, J * g + j + 1 - B)
                    last = nc.tensor.matmul(bank[j % B][:, 0:F], same[:, h, j, :], pay[:, h, j, :], start=True, stop=True)
                    if attr:
                        nc.tensor.matmul(bank[j % B][:, F:2 * F], same[:, h, j, :], attrs[:, h, j, :], start=True, stop=True)
                        last = nc.tensor.matmul(bank[j % B][:, 2 * F:2 * F + 1], same[:, h, j, :], d.ones[:, 0:1], start=True, stop=True)
                    last.then_inc(summed, 1)
                    spread(j + 2)
                pe.wait_ge(summed, J * (g + 1))
                pe.sem_inc(group_done, 1)

            loop(pe, half)

        @block.scalar
        def _(act):
            def half(i, h, first):
                g = 2 * i + h

                def make_pay(j):
                    if j >= J:
                        return
                    if j == 0:
                        act.wait_ge(rec_in[h], 16 * (i + 1))
                        if not first:
                            act.wait_ge(group_done, g - 1)
                    if windowed:
                        act.wait_ge(row_ready, J * g + j + 1)
                        row = row_bank[j % 2][:, 0:F]
                    else:
                        act.wait_ge(rows_in[h][j], 16 * (i + 1))
                        row = rows[:, h, j, :]
                    if weighted:
                        nc.scalar.activation(pay[:, h, j, :], row, ACT.Copy, scale=rec[:, h, 3, j:j + 1]).then_inc(paid, 1)
                    else:
                        nc.scalar.copy(pay[:, h, j, :], row).then_inc(paid, 1)

                make_pay(0)
                for j in range(J):
                    make_pay(j + 1)
                    act.wait_ge(summed, J * g + j + 1)
                    if not first:
                        act.wait_ge(added[j % K], 16 * (per_table * (g - 2) + j // K + 1))
                    nc.scalar.copy(sums[:, h, j, :], bank[j % B][:, 0:width]).then_inc(staged, 1)

            loop(act, half)


def gcn_nodes(nc, d):
    with ExitStack() as ctx:
        sb = lambda name, shape, dt=F32: ctx.enter_context(nc.sbuf_tensor("n1_" + name, shape, dt))
        sem = semaphores(nc, ctx, "n1_")
        acc = sb("acc", [NP, NT, F])
        part = sb("part", [NP, 2, NT, F])
        x = sb("x", [NP, NT, F])
        tile = sb("tile", [NP, 2, F])
        accT = sb("accT", [F, 2, NP])
        w = sb("w", [F, F])
        bias = sb("bias", [NP, F])
        stat = sb("stat", [NP, 3, NT])
        turned = d.bank[0:2]
        prod = d.bank[2:4]
        acc_in, x_in, w_in = sem("acc_in"), sem("x_in"), sem("w_in")
        part_in = [sem(f"part_in{b}") for b in range(2)]
        part_used = sem("part_used")
        done = sem("done")
        agg_ready = sem("agg_ready")
        turn_ready = sem("turn_ready")
        accT_ready = sem("accT_ready")
        prod_ready = sem("prod_ready")
        prod_used = sem("prod_used")
        x1_part = sem("x1_part")
        x1_ready = sem("x1_ready")
        var_ready = sem("var_ready")
        std_ready = sem("std_ready")
        h_ready = sem("h_ready")
        stored = sem("stored")
        block = ctx.enter_context(nc.Block())
        nodes = lambda t: t[0:N, :].rearrange("(p t) f -> p t f", p=NP)

        @block.sync
        def _(sp):
            sp.dma_start(acc[:], nodes(d.g)).then_inc(acc_in, 16)
            for k, t in enumerate(d.tab_gcn):
                if k >= 2:
                    sp.wait_ge(part_used, k - 1)
                sp.dma_start(part[:, k % 2, :, :], nodes(t)[:, :, 0:F]).then_inc(part_in[k % 2], 16)
            sp.dma_start(w[:], d.kernel).then_inc(w_in, 16)
            sp.dma_start(bias[:], d.bias.rearrange("(o f) -> o f", o=1).to_broadcast([NP, F])).then_inc(w_in, 16)
            sp.dma_start(x[:], nodes(d.x)).then_inc(x_in, 16)
            sp.wait_ge(x1_ready, 1)
            sp.dma_start(nodes(d.x1), x[:]).then_inc(stored, 16)
            sp.wait_ge(h_ready, 1)
            sp.dma_start(nodes(d.h1), acc[:]).then_inc(stored, 16)
            sp.wait_ge(stored, 32)

        @block.vector
        def _(dve):
            count = [0]

            def link(ins):
                count[0] += 1
                ins.then_inc(done, 1)
                dve.wait_ge(done, count[0])

            dve.wait_ge(acc_in, 16)
            for k in range(K):
                dve.wait_ge(part_in[k % 2], 16 * (k // 2 + 1))
                nc.vector.tensor_tensor(acc[:], acc[:], part[:, k % 2, :, :], ALU.add).then_inc(part_used, 1)
                dve.wait_ge(part_used, k + 1)
            dve.wait_ge(w_in, 32)
            dve.wait_ge(x_in, 16)
            with dve.Fori(0, NT // 2) as i:
                for b in range(2):
                    t = 2 * i + b
                    nc.vector.tensor_scalar(tile[:, b, :], acc[:, bass.ds(t, 1), :].rearrange("p a f -> p (a f)"),
                                            d.dinv[:, bass.ds(t, 1)], None, ALU.mult).then_inc(agg_ready, 1)
                    dve.wait_ge(prod_ready, t + 1)
                    nc.vector.tensor_tensor(part[:, b, 0, :], prod[b][0:NP, 0:F], bias[:], ALU.add).then_inc(prod_used, 1)
                    dve.wait_ge(prod_used, t + 1)
                    last = nc.vector.scalar_tensor_tensor(x[:, bass.ds(t, 1), :].rearrange("p a f -> p (a f)"), part[:, b, 0, :], 0.0,
                                                          x[:, bass.ds(t, 1), :].rearrange("p a f -> p (a f)"), ALU.max, ALU.add)
                    last.then_inc(x1_part, 1)
            dve.wait_ge(x1_part, NT)
            link(nc.vector.reduce_sum(stat[:, 0, :], x[:], AX_X))
            nc.vector.tensor_scalar(stat[:, 0, :], stat[:, 0, :], 1.0 / F, None, ALU.mult).then_inc(x1_ready, 1)
            dve.wait_ge(x1_ready, 1)
            link(nc.vector.tensor_tensor(acc[:], x[:], stat[:, 0, :].unsqueeze(2).to_broadcast([NP, NT, F]), ALU.subtract))
            link(nc.vector.tensor_tensor(part[:, 0, :, :], acc[:], acc[:], ALU.mult))
            link(nc.vector.reduce_sum(stat[:, 1, :], part[:, 0, :, :], AX_X))
            nc.vector.tensor_scalar(stat[:, 1, :], stat[:, 1, :], 1.0 / F, LN_EPS, ALU.mult, ALU.add).then_inc(var_ready, 1)
            dve.wait_ge(std_ready, 1)
            link(nc.vector.reciprocal(stat[:, 0, :], stat[:, 2, :]))
            link(nc.vector.tensor_tensor(acc[:], acc[:], stat[:, 0, :].unsqueeze(2).to_broadcast([NP, NT, F]), ALU.mult))
            nc.vector.tensor_scalar(acc[:], acc[:], 0.0, None, ALU.max).then_inc(h_ready, 1)

        @block.tensor
        def _(pe):
            pe.wait_ge(w_in, 32)
            with pe.Fori(0, NT // 2) as i:
                for b in range(2):
                    t = 2 * i + b
                    pe.wait_ge(agg_ready, t + 1)
                    nc.tensor.transpose(turned[b][:, 0:NP], tile[:, b, :], d.ident[0:NP, 0:NP]).then_inc(turn_ready, 1)
                    pe.wait_ge(accT_ready, t + 1)
                    nc.tensor.matmul(prod[b][0:NP, 0:F], accT[:, b, :], w[:], start=True, stop=True).then_inc(prod_ready, 1)
                    pe.wait_ge(prod_used, t + 1)

        @block.scalar
        def _(act):
            with act.Fori(0, NT // 2) as i:
                for b in range(2):
                    t = 2 * i + b
                    act.wait_ge(turn_ready, t + 1)
                    nc.scalar.copy(accT[:, b, :], turned[b][:, 0:NP]).then_inc(accT_ready, 1)
            act.wait_ge(var_ready, 1)
            nc.scalar.activation(stat[:, 2, :], stat[:, 1, :], ACT.Sqrt).then_inc(std_ready, 1)


def relational_sums(nc, d):
    with ExitStack() as ctx:
        sb = lambda nm, shape, dt=F32: ctx.enter_context(nc.sbuf_tensor("n2a_" + nm, shape, dt))
        sem = semaphores(nc, ctx, "n2a_")
        HT = NT // 2
        W = 2 * F + 1
        acc = sb("acc", [NP, HT, W])
        part = sb("part", [NP, 2, HT, W])
        agg = sb("agg", [NP, HT, F])
        turn_sb = sb("turn_sb", [F, 2, 2, NP])
        w = sb("w", [F, 4, F])
        bias = sb("bias", [NP, 2, F])
        cnt_dst = sb("cnt_dst", [NP, NT])
        scratch = sb("scratch", [NP, 2, F])
        turned, prod = d.bank[0:2], d.bank[2:4]
        w_in, cnt_stored, cnt_in = sem("w_in"), sem("cnt_stored"), sem("cnt_in")
        acc_in = sem("acc_in")
        part_in = [sem(f"part_in{b}") for b in range(2)]
        part_used, acc_ready = sem("part_used"), sem("acc_ready")
        turn_ready, turn_copied = sem("turn_ready"), sem("turn_copied")
        prod_ready, prod_used = sem("prod_ready"), sem("prod_used")
        agg_step, agg_ready, stored = sem("agg_step"), sem("agg_ready"), sem("stored")
        block = ctx.enter_context(nc.Block())

        def cols(t, r):
            return t[0:N, :].rearrange("(p t) f -> p t f", p=NP)[:, r * HT:(r + 1) * HT, :]

        @block.sync
        def _(sp):
            sp.dma_start(d.count_dst[0:N].rearrange("(o n) -> o n", o=1), d.row_count[0:1, 0:N]).then_inc(cnt_stored, 16)
            for m, a in enumerate((d.w_back[0:F, :], d.w_back[F:2 * F, :], d.w_fwd[0:F, :], d.w_fwd[F:2 * F, :])):
                sp.dma_start(w[:, m, :], a).then_inc(w_in, 16)
            for m, a in enumerate((d.b_back, d.b_fwd)):
                sp.dma_start(bias[:, m, :], a.rearrange("(o f) -> o f", o=1).to_broadcast([NP, F])).then_inc(w_in, 16)
            for r in range(2):
                if r:
                    sp.wait_ge(prod_used, 2 * HT)
                for k in range(K):
                    to, arrived = acc, acc_in
                    if k:
                        n = r * (K - 1) + k - 1
                        if n >= 2:
                            sp.wait_ge(part_used, n - 1)
                        to, arrived = part[:, n % 2, :, :], part_in[n % 2]
                    sp.dma_start(to[:, :, 0:F], cols(d.tab_rows[k], r)).then_inc(arrived, 16)
                    sp.dma_start(to[:, :, F:W], cols(d.tab_gcn[k], r)[:, :, F:W]).then_inc(arrived, 16)
                if r == 0:
                    sp.wait_ge(cnt_stored, 16)
                    sp.dma_start(cnt_dst[:], d.count_dst[0:N].rearrange("(p t) -> p t", p=NP)).then_inc(cnt_in, 16)
                sp.wait_ge(agg_ready, r + 1)
                sp.dma_start(cols(d.agg, r), agg[:]).then_inc(stored, 16)
                sp.wait_ge(stored, 16 * (r + 1))

        @block.vector
        def _(dve):
            dve.wait_ge(w_in, 16 * 6)
            for r in range(2):
                dve.wait_ge(acc_in, 32 * (r + 1))
                for k in range(1, K):
                    n = r * (K - 1) + k - 1
                    dve.wait_ge(part_in[n % 2], 32 * (n // 2 + 1))
                    nc.vector.tensor_tensor(acc[:], acc[:], part[:, n % 2, :, :], ALU.add).then_inc(part_used, 1)
                    dve.wait_ge(part_used, n + 1)
                if r == 0:
                    dve.wait_ge(cnt_in, 16)
                here = slice(r * HT, (r + 1) * HT)
                nc.vector.tensor_tensor(d.cnt[:, here], acc[:, :, 2 * F], cnt_dst[:, here], ALU.add).then_inc(acc_ready, 1)
                if r:
                    dve.wait_ge(stored, 16 * r)
                for tt in range(HT):
                    t = r * HT + tt
                    dve.wait_ge(prod_ready, t + 1)
                    nc.vector.scalar_tensor_tensor(scratch[:, t % 2, :], bias[:, 0, :], acc[:, tt, 2 * F:W], prod[t % 2][0:NP, 0:F],
                                                   ALU.mult, ALU.add).then_inc(prod_used, 1)
                    dve.wait_ge(prod_used, 2 * t + 1)
                    last = nc.vector.scalar_tensor_tensor(agg[:, tt, :], bias[:, 1, :], cnt_dst[:, t:t + 1], scratch[:, t % 2, :], ALU.mult, ALU.add)
                    last.then_inc(prod_used, 1)
                dve.wait_ge(prod_used, 2 * NT if r else 2 * HT)
                nc.vector.tensor_copy(scratch[:, 0, 0:1], cnt_dst[:, 0:1]).then_inc(agg_ready, 1)

        @block.tensor
        def _(pe):
            pe.wait_ge(w_in, 16 * 6)
            for t in range(NT):
                r, tt = divmod(t, HT)
                if tt == 0:
                    pe.wait_ge(acc_ready, r + 1)
                for m in range(2):
                    if t >= 2:
                        pe.wait_ge(turn_copied, 2 * (t - 2) + m + 1)
                    nc.tensor.transpose(turned[m][:, (t % 2) * P:(t % 2) * P + NP], acc[:, tt, m * F:(m + 1) * F],
                                        d.ident[0:NP, 0:NP]).then_inc(turn_ready, 1)
                if t >= 2:
                    pe.wait_ge(prod_used, 2 * (t - 1))
                out = prod[t % 2][0:NP, 0:F]
                for m, total in enumerate((d.row_sums, d.attr_sums)):
                    nc.tensor.matmul(out, total[:, t:N:NT], w[:, 2 + m, :], start=(m == 0), stop=False)
                pe.wait_ge(turn_copied, 2 * t + 2)
                for m in range(2):
                    last = nc.tensor.matmul(out, turn_sb[:, t % 2, m, :], w[:, m, :], start=False, stop=(m == 1))
                last.then_inc(prod_ready, 1)

        @block.scalar
        def _(act):
            for t in range(NT):
                for m in range(2):
                    act.wait_ge(turn_ready, 2 * t + m + 1)
                    if t >= 2:
                        act.wait_ge(prod_ready, t - 1)
                    nc.scalar.copy(turn_sb[:, t % 2, m, :], turned[m][:, (t % 2) * P:(t % 2) * P + NP]).then_inc(turn_copied, 1)


def window_sums_of_tables(nc, d):
    with ExitStack() as ctx:
        sb = lambda nm, shape, dt=F32: ctx.enter_context(nc.sbuf_tensor("fold_" + nm, shape, dt))
        sem = semaphores(nc, ctx, "fold_")
        W = 2 * F + 1
        part = sb("part", [P, K, W])
        total = sb("total", [P, W])
        loaded, added, turned, folded = sem("loaded"), sem("added"), sem("turned"), sem("folded")
        turn = d.bank[0:3]
        block = ctx.enter_context(nc.Block())

        @block.sync
        def _(sp):
            for k in range(K):
                sp.dma_start(part[:, k, :], d.tab_dst[k][0:P, :]).then_inc(loaded, 16)
            with sp.Fori(1, ROWS // P) as b:
                sp.wait_ge(folded, 3 * b)
                for k in range(K):
                    sp.dma_start(part[:, k, :], d.tab_dst[k][bass.ds(b * P, P), :]).then_inc(loaded, 16)

        @block.vector
        def _(dve):
            with dve.Fori(0, ROWS // P) as b:
                dve.wait_ge(loaded, 16 * K * (b + 1))
                nc.vector.tensor_tensor(part[:, 0, :], part[:, 0, :], part[:, 1, :], ALU.add)
                nc.vector.tensor_tensor(part[:, 2, :], part[:, 2, :], part[:, 3, :], ALU.add).then_inc(added, 1)
                dve.wait_ge(added, 2 * b + 1)
                nc.vector.tensor_tensor(total[:], part[:, 0, :], part[:, 2, :], ALU.add).then_inc(added, 1)

        @block.tensor
        def _(pe):
            with pe.Fori(0, ROWS // P) as b:
                pe.wait_ge(added, 2 * (b + 1))
                nc.tensor.transpose(turn[0][:, 0:P], total[:, 0:F], d.ident[:])
                nc.tensor.transpose(turn[1][:, 0:P], total[:, F:2 * F], d.ident[:])
                nc.tensor.transpose(turn[2][0:1, 0:P], total[:, 2 * F:W], d.ident[:]).then_inc(turned, 1)

        @block.scalar
        def _(act):
            with act.Fori(0, ROWS // P) as b:
                act.wait_ge(turned, b + 1)
                at = bass.ds(b * P, P)
                nc.scalar.copy(d.row_sums[:, at], turn[0][:, 0:P]).then_inc(folded, 1)
                nc.scalar.copy(d.attr_sums[:, at], turn[1][:, 0:P]).then_inc(folded, 1)
                nc.scalar.copy(d.row_count[0:1, at], turn[2][0:1, 0:P]).then_inc(folded, 1)
                act.wait_ge(folded, 3 * (b + 1))


def last_nodes(nc, d):
    with ExitStack() as ctx:
        sb = lambda name, shape, dt=F32: ctx.enter_context(nc.sbuf_tensor("n2_" + name, shape, dt))
        sem = semaphores(nc, ctx, "n2_")
        agg = sb("agg", [NP, NT, F])
        h1 = sb("h1", [NP, NT, F])
        x1 = sb("x1", [NP, NT, F])
        work = sb("work", [NP, NT, F])
        gamma = sb("gamma", [NP, F])
        beta = sb("beta", [NP, F])
        stat = sb("stat", [NP, 3, NT])
        agg_in, loaded, done = sem("agg_in"), sem("loaded"), sem("done")
        var_ready, std_ready = sem("var_ready"), sem("std_ready")
        out_ready, stored = sem("out_ready"), sem("stored")
        block = ctx.enter_context(nc.Block())
        nodes = lambda t: t[0:N, :].rearrange("(p t) f -> p t f", p=NP)

        @block.sync
        def _(sp):
            sp.dma_start(agg[:], nodes(d.agg)).then_inc(agg_in, 16)
            sp.dma_start(h1[:], nodes(d.h1)).then_inc(loaded, 16)
            sp.dma_start(x1[:], nodes(d.x1)).then_inc(loaded, 16)
            for a, t in ((d.gamma, gamma), (d.beta, beta)):
                sp.dma_start(t[:], a.rearrange("(o f) -> o f", o=1).to_broadcast([NP, F])).then_inc(loaded, 16)
            sp.wait_ge(out_ready, 1)
            sp.dma_start(nodes(d.out), work[:]).then_inc(stored, 16)
            sp.wait_ge(stored, 16)

        @block.scalar
        def _(act):
            act.wait_ge(var_ready, 1)
            nc.scalar.activation(stat[:, 2, :], stat[:, 1, :], ACT.Sqrt).then_inc(std_ready, 1)

        @block.vector
        def _(dve):
            count = [0]

            def link(ins):
                count[0] += 1
                ins.then_inc(done, 1)
                dve.wait_ge(done, count[0])

            per_node = lambda r: stat[:, r, :].unsqueeze(2).to_broadcast([NP, NT, F])
            per_feature = lambda a: a[:].unsqueeze(1).to_broadcast([NP, NT, F])
            link(nc.vector.tensor_scalar(stat[:, 0, :], d.cnt[:], AGG_EPS, None, ALU.add))
            link(nc.vector.reciprocal(stat[:, 1, :], stat[:, 0, :]))
            dve.wait_ge(agg_in, 16)
            link(nc.vector.tensor_tensor(agg[:], agg[:], per_node(1), ALU.mult))
            link(nc.vector.scalar_tensor_tensor(agg[:], agg[:], SLOPE, agg[:], ALU.mult, ALU.max))
            dve.wait_ge(loaded, 64)
            link(nc.vector.tensor_tensor(agg[:], agg[:], h1[:], ALU.add))
            link(nc.vector.reduce_sum(stat[:, 0, :], agg[:], AX_X))
            link(nc.vector.tensor_scalar(stat[:, 0, :], stat[:, 0, :], 1.0 / F, None, ALU.mult))
            link(nc.vector.tensor_tensor(agg[:], agg[:], per_node(0), ALU.subtract))
            link(nc.vector.tensor_tensor(work[:], agg[:], agg[:], ALU.mult))
            link(nc.vector.reduce_sum(stat[:, 1, :], work[:], AX_X))
            nc.vector.tensor_scalar(stat[:, 1, :], stat[:, 1, :], 1.0 / F, LN_EPS, ALU.mult, ALU.add).then_inc(var_ready, 1)
            dve.wait_ge(std_ready, 1)
            link(nc.vector.reciprocal(stat[:, 0, :], stat[:, 2, :]))
            link(nc.vector.tensor_tensor(agg[:], agg[:], per_feature(gamma), ALU.mult))
            link(nc.vector.tensor_tensor(agg[:], agg[:], per_node(0), ALU.mult))
            link(nc.vector.tensor_tensor(agg[:], agg[:], per_feature(beta), ALU.add))
            nc.vector.tensor_tensor(work[:], agg[:], x1[:], ALU.add).then_inc(out_ready, 1)


def program(nc, d):
    dram = lambda name, shape, dt=F32: nc.dram_tensor(name, shape, dt).ap()
    d.src_i, d.dst_i = dram("src_pad", (EP,), I32), dram("dst_pad", (EP,), I32)
    d.src_f, d.dst_f, d.rel_f = dram("src_key", (EP,)), dram("dst_key", (EP,)), dram("dst_offset", (EP,))
    d.rec = dram("edge_records", (NG, P, REC * J))
    d.g, d.h1, d.x1 = dram("g", (ROWS, F)), dram("h1", (ROWS, F)), dram("x1", (ROWS, F))
    d.agg, d.count_dst = dram("agg", (ROWS, F)), dram("count_dst", (ROWS,))
    d.tab_gcn = [dram(f"gcn_sums{k}", (ROWS, 2 * F + 1)) for k in range(K)]
    d.tab_rows = [dram(f"row_sums{k}", (ROWS, F)) for k in range(K)]
    d.tab_dst = [dram(f"dst_sums{k}", (ROWS, 2 * F + 1)) for k in range(K)]
    d.cleared = d.tab_gcn + d.tab_rows + d.tab_dst
    with ExitStack() as ctx:
        sb = lambda name, shape, dt=F32: ctx.enter_context(nc.sbuf_tensor(name, shape, dt))
        d.dinv = sb("dinv", [NP, NT])
        d.cnt = sb("cnt", [NP, NT])
        d.ident = sb("ident", [P, P])
        d.ones = sb("ones", [P, P])
        d.iota = sb("iota", [P, P])
        d.part_i = sb("part_i", [P, J], I32)
        d.part = sb("part", [P, J])
        d.before_me = sb("before_me", [P, P])
        d.spare = sb("spare", [P, J])
        d.base_i = sb("base_i", [1, NG], I32)
        d.windowed = sb("windowed", [1, 1], I32)
        d.bank = [ctx.enter_context(nc.psum_tensor(f"bank{b}", [P, 512], F32)) for b in range(8)]
        with ExitStack() as inner:
            wide = lambda name, rows: inner.enter_context(nc.sbuf_tensor(name, [rows, ROWS], F32))
            d.attr_sums, d.row_sums, d.row_count = wide("attr_sums", F), wide("row_sums", F), wide("row_count", 1)
            setup_and_degrees(nc, d)
            windowed = nc.values_load(d.windowed[0:1, 0:1], min_val=0, max_val=1)
            with nc.If(windowed == 1):
                edge_pass(nc, d, "gw", d.g, None, 0, d.tab_gcn, weighted=True, attr=True, window_sums="attr")
            with nc.Else():
                edge_pass(nc, d, "gg", d.g, d.dst_i, 0, d.tab_gcn, weighted=True, attr=True)
            gcn_nodes(nc, d)
            windowed = nc.values_load(d.windowed[0:1, 0:1], min_val=0, max_val=1)
            with nc.If(windowed == 1):
                edge_pass(nc, d, "rw", d.h1, None, 0, d.tab_rows, window_sums="rows", sums_rows_at=d.src_i)
            with nc.Else():
                edge_pass(nc, d, "rs", d.h1, d.dst_i, 0, d.tab_rows)
                edge_pass(nc, d, "rd", d.h1, d.src_i, 1, d.tab_dst, attr=True)
                window_sums_of_tables(nc, d)
            relational_sums(nc, d)
        last_nodes(nc, d)


INPUTS = {"x": "x", "src": "src", "dst": "dst", "edge_attr_128": "edge_attr", "edge_weight": "w", "L0_gnn_kernel": "kernel",
          "L0_gnn_bias": "bias", "L1_gnn_W_fwd": "w_fwd", "L1_gnn_b_fwd": "b_fwd", "L1_gnn_W_back": "w_back",
          "L1_gnn_b_back": "b_back", "L1_gnn_gamma": "gamma", "L1_gnn_beta": "beta"}


def kernel(**inputs):
    import concourse.bacc as bacc
    from concourse.bass_utils import run_bass_kernel_spmd as run

    nc = bacc.Bacc("TRN2", target_bir_lowering=False, num_devices=1)
    d = Net()
    arrays = {}
    for name, short in INPUTS.items():
        a = np.ascontiguousarray(inputs[name])
        arrays[f"in_{name}"] = a
        d.__dict__[short] = nc.dram_tensor(f"in_{name}", a.shape, mybir.dt.from_np(a.dtype), kind="ExternalInput").ap()
    d.out = nc.dram_tensor("out", (N, F), F32, kind="ExternalOutput").ap()
    program(nc, d)
    return run(nc, [arrays], core_ids=[0]).results[0]["out"]
```

```python
from contextlib import ExitStack

import numpy as np
import concourse.bass as bass
from concourse import mybir

F32 = mybir.dt.float32
BF16 = mybir.dt.bfloat16
I16 = mybir.dt.int16
I32 = mybir.dt.int32
ALU = mybir.AluOpType
ACT = mybir.ActivationFunctionType
AX_X = mybir.AxisListType.X

N = 6250
E = 206250
F = 128
P = 128
NP, NT = 125, 50
J = 8
GE = P * J
NG = 2 * -(-E // (2 * GE))
EP = NG * GE
FULL = E // GE
EC = EP // P
ROWFULL, ROWTAIL = divmod(E, EC)
TAILP, TAILJ = divmod(E - FULL * GE, J)
PADKEY = N
SPARE = N + 1
ROWS = 6400
REC = 4
K = 8
LN_EPS = 1e-5
AGG_EPS = 1e-7
SLOPE = 0.01
WJ = 2 * J
SLOTS = 64
STEP = 4
NEAR = E // STEP + 1
TILES = ROWS // P
HI = -(-N // P)
SUPER = TILES // 2
PAIRS = P
HH = 2 * HI
ROUND = 12582912.0


def semaphores(nc, ctx, prefix):
    taken = []

    def sem(name):
        taken.append(nc.alloc_semaphore(prefix + name))
        return taken[-1]

    def clear():
        nc.clear_and_free_semaphores(taken)
        nc.all_engine_barrier()

    ctx.callback(clear)
    return sem


class Net:
    pass


def setup_and_degrees(nc, d):
    with ExitStack() as ctx:
        sb = lambda name, shape, dt=F32: ctx.enter_context(nc.sbuf_tensor(name, shape, dt))
        sem = semaphores(nc, ctx, "setup_")
        CUT = 10
        zeros = sb("zeros", [P, ROWS // P // CUT * 2 * F])
        src_i = sb("src_i", [P, EC], I32)
        dst_i = sb("dst_i", [P, EC], I32)
        src_run, dst_run, w_run = (d.attr_sums[:, r * EC:(r + 1) * EC] for r in range(3))
        key16 = sb("key16", [P, 2, EC], I16)
        rel16 = sb("rel16", [P, NG, J], BF16)
        rec = sb("rec", [P, NG, REC, J])
        row_f = sb("row_f", [P, EC])
        row_of = sb("row_of", [P, 2, EC], BF16)
        col_of = sb("col_of", [P, 2, EC], BF16)
        w_parts = sb("w_parts", [P, 2, EC], BF16)
        numbers = sb("numbers", [P, P, WJ], BF16)
        base_b = sb("base_b", [P, NG])
        wide = sb("wide", [P, 4])
        iota_i = sb("iota_i", [P, P], I32)
        row_hot = sb("row_hot", [P, 2, 2, NP, WJ], BF16)
        col_hot = sb("col_hot", [P, 2, NT, WJ], BF16)
        col_w = sb("col_w", [P, 2, 4, NT, WJ], BF16)
        deg = sb("deg", [NP, NT])
        has_edge = sb("has_edge", [NP, NT])
        x = sb("x_sb", [NP, NT, F])
        xc = sb("xc", [NP, NT, F])
        stat = sb("stat", [NP, 3, NT])
        src_f, dst_f, rel_f, w_f = (rec[:, :, r, :] for r in range(REC))
        hist, hist_dst, spread = d.bank[0:3]
        edges_in = sem("edges_in")
        x_in = sem("x_in")
        zeroed = sem("zeroed")
        pads = sem("pads")
        iota_ready = sem("iota_ready")
        ident_ready = sem("ident_ready")
        done = sem("done")
        runs_ready, runs_read, runs_stored = sem("runs_ready"), sem("runs_read"), sem("runs_stored")
        rec_in = sem("rec_in")
        base_ready = sem("base_ready")
        wide_ready = sem("wide_ready")
        wide_summed = sem("wide_summed")
        rec_ready = sem("rec_ready")
        var_ready = sem("var_ready")
        std_ready = sem("std_ready")
        g_ready = sem("g_ready")
        hot_ready = sem("hot_ready")
        hist_ready = sem("hist_ready")
        sums_ready, mean_ready, scale_ready, normed = sem("sums_ready"), sem("mean_ready"), sem("scale_ready"), sem("normed")
        hot_used, parts_ready, second_ready, third_ready = sem("hot_used"), sem("parts_ready"), sem("second_ready"), sem("third_ready")
        step = sem("step")
        stored = sem("stored")
        cleared = sem("cleared")
        ROWS_EACH = 5
        AT = 14
        SECTIONS = ((1, AT, "offsets"), (AT, AT + NT // ROWS_EACH, "deviations"),
                    (AT + NT // ROWS_EACH, AT + 2 * NT // ROWS_EACH, None), (AT + 2 * NT // ROWS_EACH, NG // 4, None))
        block = ctx.enter_context(nc.Block())

        @block.sync
        def _(sp):
            sp.wait_ge(pads, 3)
            for a, t in ((d.src, src_i), (d.dst, dst_i), (d.w, w_run)):
                sp.dma_start(t[0:ROWFULL, :], a[0:ROWFULL * EC].rearrange("(p c) -> p c", c=EC)).then_inc(edges_in, 16)
                sp.dma_start(t[ROWFULL:ROWFULL + 1, 0:ROWTAIL], a[ROWFULL * EC:E].rearrange("(p c) -> p c", p=1)).then_inc(edges_in, 16)
            sp.dma_start(x[:], d.x.rearrange("(p t) f -> p t f", p=NP)).then_inc(x_in, 16)
            sp.wait_ge(runs_ready, 4)
            for a, t in ((d.src_f, src_run), (d.dst_f, dst_run), (d.w_f, w_run), (d.src_i, src_i[:]), (d.dst_i, dst_i[:]),
                         (d.src_key, key16[:, 0, :]), (d.dst_key, key16[:, 1, :])):
                sp.dma_start(a.rearrange("(p c) -> p c", c=EC), t).then_inc(runs_stored, 16)
            sp.wait_ge(runs_stored, 16 * 7)
            groups = lambda a: a.rearrange("(g p j) -> p g j", p=P, j=J)
            for a, t in ((d.dst_f, dst_f), (d.src_f, src_f), (d.w_f, w_f)):
                sp.dma_start(t, groups(a)).then_inc(rec_in, 16)
            sp.dma_start(d.near, bass.AP(d.src_f.tensor, 0, [[STEP, NEAR], [1, SLOTS]])).then_inc(stored, 16)
            sp.wait_ge(zeroed, 1)
            for t in d.tab_gcn:
                view = t.rearrange("(p q r) c -> p q (r c)", p=P, q=CUT)
                for q in range(CUT):
                    sp.dma_start(view[:, q, :], zeros[:]).then_inc(cleared, 16)
            for t in (d.g, d.h1):
                sp.dma_start(t[N:ROWS, :].rearrange("(p r) f -> p (r f)", r=2), zeros[0:(ROWS - N) // 2, 0:2 * F]).then_inc(cleared, 16)
            sp.wait_ge(rec_ready, 2)
            sp.dma_start(groups(d.dst_offset), rel16[:]).then_inc(stored, 16)
            sp.dma_start(d.rec.rearrange("g p r -> p g r"), rec[:].rearrange("p g r j -> p g (r j)")).then_inc(stored, 16)
            sp.wait_ge(g_ready, 1)
            sp.dma_start(d.g[0:N, :].rearrange("(p t) f -> p t f", p=NP), xc[:]).then_inc(stored, 16)
            sp.wait_ge(stored, 16 * 4)
            sp.wait_ge(cleared, 16 * (CUT * K + 2))

        @block.gpsimd
        def _(pool):
            nc.gpsimd.memset(d.ident[:], 0.0).then_inc(ident_ready, 1)
            nc.gpsimd.memset(d.ones[:], 1.0).then_inc(iota_ready, 1)
            nc.gpsimd.iota(iota_i[:], pattern=[[1, P]], base=0, channel_multiplier=0).then_inc(iota_ready, 1)
            nc.gpsimd.iota(d.part_i[:], pattern=[[0, J]], base=0, channel_multiplier=1).then_inc(iota_ready, 1)
            pool.wait_ge(ident_ready, 1)
            nc.gpsimd.affine_select(out=d.ident[:], in_=d.ident[:], compare_op=ALU.not_equal, fill=1.0, base=0,
                                    pattern=[[-1, P]], channel_multiplier=1).then_inc(ident_ready, 1)
            pool.wait_ge(ident_ready, 2)
            nc.gpsimd.memset(zeros[:], 0.0).then_inc(zeroed, 1)
            pool.wait_ge(runs_read, 1)
            pool.wait_ge(runs_stored, 16 * 7)
            nc.gpsimd.memset(d.attr_sums[:], 0.0).then_inc(ident_ready, 1)

            def seconds(i, h, first):
                n = 2 * i + h
                pool.wait_ge(step, 2 * n + 1)
                if not first:
                    pool.wait_ge(hot_used, n - 1)
                nc.gpsimd.tensor_tensor(col_w[:, h, 1, :, :], col_w[:, h, 3, :, :],
                                        w_parts[:, 1, bass.ds(WJ * n, WJ)].unsqueeze(1).to_broadcast([P, NT, WJ]), ALU.mult).then_inc(second_ready, 1)

            pool.wait_ge(parts_ready, 1)
            seconds(0, 0, True)
            seconds(0, 1, True)
            with pool.Fori(1, NG // 4) as i:
                seconds(i, 0, False)
                seconds(i, 1, False)
            seconds(NG // 4, 0, False)

        @block.scalar
        def _(act):
            act.wait_ge(x_in, 16)
            for t in range(NT):
                nc.scalar.activation(xc[:, t, :], x[:, t, :], ACT.Copy, accum_out=stat[:, 0, t:t + 1]).then_inc(sums_ready, 1)

            def thirds(i, h, first):
                n = 2 * i + h
                act.wait_ge(step, 2 * n + 1)
                if not first:
                    act.wait_ge(hot_used, n - 1)
                for j in range(WJ):
                    nc.scalar.activation(col_w[:, h, 2, :, j], col_w[:, h, 3, :, j], ACT.Copy,
                                         scale=row_f[:, bass.ds(WJ * n + j, 1)]).then_inc(third_ready, 1)

            def squares(t):
                at = bass.ds(t, 1)
                nc.scalar.activation(xc[:, at, :], x[:, at, :], ACT.Square, bias=stat[:, 0, at], accum_out=stat[:, 1, at]).then_inc(sums_ready, 1)

            def normed_row(t):
                at = bass.ds(t, 1)
                nc.scalar.activation(xc[:, at, :], x[:, at, :], ACT.Relu, bias=stat[:, 0, at], scale=stat[:, 1, at]).then_inc(normed, 1)

            thirds(0, 0, True)
            thirds(0, 1, True)
            for (begin, end, then), row in zip(SECTIONS, (None, squares, normed_row, None)):
                if row is squares:
                    act.wait_ge(mean_ready, 1)
                if row is normed_row:
                    act.wait_ge(var_ready, 1)
                    nc.scalar.activation(stat[:, 2, :], stat[:, 1, :], ACT.Sqrt).then_inc(std_ready, 1)
                    act.wait_ge(scale_ready, 1)
                with act.Fori(begin, end) as i:
                    thirds(i, 0, False)
                    thirds(i, 1, False)
                    for k in range(ROWS_EACH if row else 0):
                        row(ROWS_EACH * (i - begin) + k)
            thirds(NG // 4, 0, False)
            act.wait_ge(var_ready, 2)
            nc.scalar.activation(stat[:, 2, :], deg[:], ACT.Sqrt).then_inc(std_ready, 1)

        @block.vector
        def _(dve):
            count = [0]

            def link(ins):
                count[0] += 1
                ins.then_inc(done, 1)
                dve.wait_ge(done, count[0])

            nc.vector.memset(src_i[:, ROWTAIL:], PADKEY).then_inc(pads, 1)
            nc.vector.memset(dst_i[:, ROWTAIL:], PADKEY).then_inc(pads, 1)
            nc.vector.memset(w_run[:, ROWTAIL:], 0.0).then_inc(pads, 1)
            nc.vector.memset(deg[:], 1.0)
            dve.wait_ge(iota_ready, 3)
            nc.vector.tensor_copy(d.iota[:], iota_i[:])
            link(nc.vector.tensor_copy(d.part[:], d.part_i[:]))
            nc.vector.tensor_tensor(d.before_me[:], d.iota[:], d.part[:, 0:1].to_broadcast([P, P]), ALU.is_lt)
            link(nc.vector.tensor_scalar(d.spare[:], d.part[:], float(SPARE), None, ALU.add))
            dve.wait_ge(edges_in, 16 * 6)
            nc.vector.tensor_copy(src_run, src_i[:]).then_inc(runs_ready, 1)
            nc.vector.tensor_copy(dst_run, dst_i[:]).then_inc(runs_ready, 1)
            nc.vector.tensor_copy(key16[:, 0, :], src_i[:]).then_inc(runs_ready, 1)
            nc.vector.tensor_copy(key16[:, 1, :], dst_i[:]).then_inc(runs_ready, 1)
            dve.wait_ge(runs_ready, 4)
            for m, node in enumerate((src_run, dst_run)):
                link(nc.vector.tensor_scalar(row_f[:], node, 1.0 / NT, 0.5 / NT - 0.5, ALU.mult, ALU.add))
                link(nc.vector.tensor_scalar(row_f[:], row_f[:], ROUND, ROUND, ALU.add, ALU.subtract))
                nc.vector.tensor_copy(row_of[:, m, :], row_f[:])
                link(nc.vector.scalar_tensor_tensor(col_of[:, m, :], row_f[:], -float(NT), node, ALU.mult, ALU.add))
            link(nc.vector.tensor_copy(w_parts[:, 0, :], w_run))
            nc.vector.tensor_tensor(row_f[:], w_run, w_parts[:, 0, :], ALU.subtract).then_inc(runs_read, 1)
            dve.wait_ge(runs_read, 1)
            link(nc.vector.tensor_copy(w_parts[:, 1, :], row_f[:]))
            link(nc.vector.tensor_tensor(row_f[:], row_f[:], w_parts[:, 1, :], ALU.subtract))
            nc.vector.tensor_copy(numbers[:], d.iota[:].unsqueeze(2).to_broadcast([P, P, WJ])).then_inc(parts_ready, 1)
            dve.wait_ge(parts_ready, 1)

            def offsets():
                dve.wait_ge(base_ready, 1)
                link(nc.vector.tensor_copy(base_b[:], spread[:, 0:NG]))
                nc.vector.tensor_copy(d.base_i[:], base_b[0:1, :])
                nc.vector.tensor_tensor(rel_f, dst_f, base_b[:].unsqueeze(2).to_broadcast([P, NG, J]), ALU.subtract).then_inc(rec_ready, 1)
                dve.wait_ge(rec_ready, 1)
                nc.vector.tensor_copy(rel16[:], rel_f).then_inc(rec_ready, 1)
                nc.vector.tensor_reduce(wide[:, 0:1], rel_f, mybir.AxisListType.XY, ALU.max)
                link(nc.vector.tensor_reduce(wide[:, 1:2], rel_f, mybir.AxisListType.XY, ALU.min))
                nc.vector.tensor_scalar(wide[:, 0:1], wide[:, 0:1], P - 0.5, None, ALU.is_gt)
                link(nc.vector.tensor_scalar(wide[:, 1:2], wide[:, 1:2], -0.5, None, ALU.is_lt))
                nc.vector.tensor_tensor(wide[:, 2:3], wide[:, 0:1], wide[:, 1:2], ALU.max).then_inc(wide_ready, 1)
                dve.wait_ge(sums_ready, NT)
                nc.vector.tensor_scalar(stat[:, 0, :], stat[:, 0, :], -1.0 / F, None, ALU.mult).then_inc(mean_ready, 1)

            def deviations():
                dve.wait_ge(wide_summed, 1)
                nc.vector.tensor_scalar(d.windowed[:], spread[0:1, 256:257], 0.5, None, ALU.is_lt)
                dve.wait_ge(sums_ready, 2 * NT)
                nc.vector.tensor_scalar(stat[:, 1, :], stat[:, 1, :], 1.0 / F, LN_EPS, ALU.mult, ALU.add).then_inc(var_ready, 1)
                dve.wait_ge(std_ready, 1)
                link(nc.vector.reciprocal(stat[:, 1, :], stat[:, 2, :]))
                nc.vector.tensor_tensor(stat[:, 0, :], stat[:, 0, :], stat[:, 1, :], ALU.mult).then_inc(scale_ready, 1)

            def one_hots(i, h):
                n = 2 * i + h
                pair = lambda t: t[:, bass.ds(WJ * n, WJ)].unsqueeze(1)
                for m, cols in enumerate((col_w[:, h, 3, :, :], col_hot[:, h, :, :])):
                    nc.vector.tensor_tensor(cols, numbers[:, 0:NT, :], pair(col_of[:, m, :]).to_broadcast([P, NT, WJ]),
                                            ALU.is_equal).then_inc(step, 1)
                    nc.vector.tensor_tensor(row_hot[:, h, m, :, :], numbers[:, 0:NP, :], pair(row_of[:, m, :]).to_broadcast([P, NP, WJ]),
                                            ALU.is_equal)
                dve.wait_ge(step, 2 * n + 1)
                nc.vector.tensor_tensor(col_w[:, h, 0, :, :], col_w[:, h, 3, :, :], pair(w_parts[:, 0, :]).to_broadcast([P, NT, WJ]),
                                        ALU.mult).then_inc(hot_ready, 1)

            one_hots(0, 0)
            one_hots(0, 1)
            for begin, end, then in SECTIONS:
                with dve.Fori(begin, end) as i:
                    for h in range(2):
                        dve.wait_ge(hot_used, 2 * i + h - 1)
                        one_hots(i, h)
                if then == "offsets":
                    offsets()
                if then == "deviations":
                    deviations()
            dve.wait_ge(hot_used, NG // 2 - 2)
            one_hots(NG // 4, 0)
            dve.wait_ge(hist_ready, 1)
            nc.vector.tensor_copy(d.cnt_src[:], hist[0:NP, 3 * NT:4 * NT])
            link(nc.vector.tensor_copy(d.cnt_dst[:], hist_dst[0:NP, 0:NT]))
            nc.vector.tensor_tensor(d.cnt[:], d.cnt_src[:], d.cnt_dst[:], ALU.add)
            for part in range(3):
                link(nc.vector.tensor_tensor(deg[:], deg[:], hist[0:NP, part * NT:(part + 1) * NT], ALU.add))

            link(nc.vector.tensor_scalar(has_edge[:], deg[:], 0.0, None, ALU.is_gt))
            nc.vector.tensor_scalar(deg[:], deg[:], 1e-30, None, ALU.max).then_inc(var_ready, 1)
            dve.wait_ge(std_ready, 2)
            link(nc.vector.reciprocal(stat[:, 0, :], stat[:, 2, :]))
            link(nc.vector.tensor_tensor(d.dinv[:], stat[:, 0, :], has_edge[:], ALU.mult))
            dve.wait_ge(normed, NT)
            nc.vector.tensor_tensor(xc[:], xc[:], d.dinv[:].unsqueeze(2).to_broadcast([NP, NT, F]), ALU.mult).then_inc(g_ready, 1)

        @block.tensor
        def _(pe):
            def offsets():
                pe.wait_ge(rec_in, 16 * 3)
                pe.wait_ge(iota_ready, 3)
                nc.tensor.matmul(spread[:, 0:NG], d.ones[0:1, :], dst_f[0:1, :, 0], start=True, stop=True).then_inc(base_ready, 1)
                pe.wait_ge(wide_ready, 1)
                nc.tensor.matmul(spread[0:1, 256:257], wide[:, 2:3], d.ones[:, 0:1], start=True, stop=True).then_inc(wide_summed, 1)

            def chunks(i, h, first, last):
                pe.wait_ge(hot_ready, 2 * i + h + 1)
                pe.wait_ge(second_ready, 2 * i + h + 1)
                pe.wait_ge(third_ready, WJ * (2 * i + h + 1))
                for j in range(WJ):
                    ends = dict(start=first and j == 0, stop=last and j == WJ - 1)
                    nc.tensor.matmul(hist[0:NP, 0:4 * NT], row_hot[:, h, 0, :, j], col_w[:, h, :, :, j].rearrange("p s n -> p (s n)"), **ends)
                    done_with = nc.tensor.matmul(hist_dst[0:NP, 0:NT], row_hot[:, h, 1, :, j], col_hot[:, h, :, j], **ends)
                done_with.then_inc(hist_ready if last else hot_used, 1)

            chunks(0, 0, True, False)
            chunks(0, 1, False, False)
            for begin, end, then in SECTIONS:
                with pe.Fori(begin, end) as i:
                    chunks(i, 0, False, False)
                    chunks(i, 1, False, False)
                if then == "offsets":
                    offsets()
            chunks(NG // 4, 0, False, True)


def edge_pass(nc, d, name, rows_from, row_at, key_row, tables, weighted=False, attr=False, window_sums=False):
    width = tables[0].shape[1]
    windowed = row_at is None
    key_lin = (d.src_key, d.dst_key)[key_row]
    with ExitStack() as ctx:
        sb = lambda nm, shape, dt=F32: ctx.enter_context(nc.sbuf_tensor(f"{name}_{nm}", shape, dt))
        sem = semaphores(nc, ctx, name + "_")
        rec = sb("rec", [P, 2, REC, J])
        key_b = sb("key_b", [P, 2, P, J], I16)
        same = sb("same", [P, 2, J, P])
        earlier = sb("earlier", [P, J, P])
        before = sb("before", [P, J])
        to_f = sb("to_f", [P, J])
        to_i = sb("to_i", [P, 2, J], I32)
        pay = sb("pay", [P, 2, J, F])
        sums = sb("sums", [P, 2, J, width])
        if not windowed:
            at_i = sb("at_i", [P, 2, J], I32)
            rows = sb("rows", [P, 2, J, F])
        if attr:
            attrs = sb("attrs", [P, 2, J, F])
        if windowed:
            rel_b = sb("rel_b", [P, 2, P, J], BF16)
            window = sb("window", [P, 2, F])
            spread_hot = sb("spread_hot", [P, 2, J, P])
            sum_hot = sb("sum_hot", [P, 2, J, P])
        B = 4
        bank, row_bank, win_bank = d.bank[0:B], d.bank[4:6], d.bank[6:8]
        rec_in = [sem(f"rec_in{h}") for h in range(2)]
        key_in = [sem(f"key_in{h}") for h in range(2)]
        at_in = [sem(f"at_in{h}") for h in range(2)]
        attr_in = [sem(f"attr_in{h}") for h in range(2)]
        tail_in = sem("tail_in")
        rel_in = [sem(f"rel_in{h}") for h in range(2)]
        window_in = [sem(f"window_in{h}") for h in range(2)]
        rows_in = [[sem(f"rows_in{h}_{j}") for j in range(J)] for h in range(2)] if not windowed else None
        spread_ready, same_ready, sum_ready = sem("spread_ready"), sem("same_ready"), sem("sum_ready")
        step, to_ready = sem("step"), sem("to_ready")
        row_ready = sem("row_ready")
        paid = sem("paid")
        summed = sem("summed")
        group_done = sem("group_done")
        window_added = sem("window_added")
        staged = sem("staged")
        turns, load_turns = sem("turns"), sem("load_turns")
        added = [sem(f"added{k}") for k in range(K)]
        per_table = J // K
        LAST = NG // 2 - 1
        block = ctx.enter_context(nc.Block())

        def loop(eng, half):
            half(0, 0, True)
            half(0, 1, True)
            with eng.Fori(1, LAST) as i:
                half(i, 0, False)
                half(i, 1, False)
            half(LAST, 0, False)
            half(LAST, 1, False)

        def group_at(g):
            return slice(g * GE, (g + 1) * GE) if isinstance(g, int) else bass.ds(g * GE, GE)

        @block.sync
        def _(sp):
            def half(i, h, first):
                g = 2 * i + h
                if not first:
                    sp.wait_ge(to_ready, g - 1)
                    sp.sem_inc(load_turns, 1)
                    sp.wait_ge(paid, J * (g - 1))
                    sp.sem_inc(load_turns, 1)
                everywhere = lambda a: a[group_at(g)].rearrange("(o e) -> o e", o=1).to_broadcast([P, GE])
                flat = lambda t: t[:, h, :, :].rearrange("p q j -> p (q j)")
                sp.dma_start(rec[:, h, :, :].rearrange("p r j -> p (r j)"),
                             d.rec[bass.ds(g, 1), :, :].rearrange("o p r -> (o p) r")).then_inc(rec_in[h], 16)
                if windowed:
                    sp.dma_start(flat(rel_b), everywhere(d.dst_offset)).then_inc(rel_in[h], 16)
                sp.dma_start(flat(key_b), everywhere(key_lin)).then_inc(key_in[h], 16)
                if not first:
                    sp.wait_ge(group_done, g - 1)
                    sp.sem_inc(load_turns, 1)
                if windowed:
                    base = sp.value_load(d.base_i[0:1, bass.ds(g, 1)], min_val=0, max_val=N)
                    sp.dma_start(window[:, h, :], rows_from[bass.ds(base, P), :]).then_inc(window_in[h], 16)
                if not windowed:
                    sp.dma_start(at_i[:, h, :], row_at[group_at(g)].rearrange("(p j) -> p j", j=J)).then_inc(at_in[h], 16)
                if attr and not (isinstance(g, int) and g == FULL):
                    sp.dma_start(flat(attrs), d.edge_attr[group_at(g), :].rearrange("(p j) f -> p (j f)", j=J)).then_inc(attr_in[h], 16)
                if attr and isinstance(g, int) and g == FULL:
                    at = g * GE + TAILP * J
                    sp.dma_start(flat(attrs[0:TAILP]), d.edge_attr[g * GE:at, :].rearrange("(p j) f -> p (j f)", j=J)).then_inc(attr_in[h], 16)
                    sp.dma_start(attrs[TAILP:TAILP + 1, h, 0:TAILJ, :].rearrange("p j f -> p (j f)"),
                                 d.edge_attr[at:E, :].rearrange("(p j) f -> p (j f)", p=1)).then_inc(tail_in, 16)

            loop(sp, half)

        @block.gpsimd
        def _(pool):
            def gather(i, h, j, first):
                g = 2 * i + h
                if windowed:
                    return
                if j == 0:
                    pool.wait_ge(at_in[h], 16 * (i + 1))
                    if not first:
                        pool.wait_ge(group_done, g - 1)
                        pool.wait_ge(paid, J * (g - 1))
                    pool.sem_inc(turns, 1)
                nc.gpsimd.indirect_dma_start(
                    out=rows[:, h, j, :], out_offset=None, in_=rows_from,
                    in_offset=bass.IndirectOffsetOnAxis(ap=at_i[:, h, j:j + 1], axis=0)).then_inc(rows_in[h][j], 16)

            def scatter(i, h, j, first):
                g = 2 * i + h
                if j == 0:
                    pool.wait_ge(to_ready, g + 1)
                pool.wait_ge(staged, J * g + j + 1)
                if not (first and h == 0 and j < K):
                    pool.wait_ge(added[j % K], 16 * (per_table * g + j // K))
                pool.sem_inc(turns, 1)
                nc.gpsimd.indirect_dma_start(
                    out=tables[j % K], out_offset=bass.IndirectOffsetOnAxis(ap=to_i[:, h, j:j + 1], axis=0),
                    in_=sums[:, h, j, :], in_offset=None, compute_op=ALU.add).then_inc(added[j % K], 16)

            for j in range(J):
                gather(0, 0, j, True)
            for j in range(J):
                gather(0, 1, j, True)
                scatter(0, 0, j, True)
            with pool.Fori(1, NG // 2) as i:
                for j in range(J):
                    gather(i, 0, j, False)
                    scatter(i - 1, 1, j, False)
                for j in range(J):
                    gather(i, 1, j, False)
                    scatter(i, 0, j, False)
            for j in range(J):
                scatter(LAST, 1, j, False)
            for k in range(K):
                pool.wait_ge(added[k], 16 * per_table * NG)

        @block.vector
        def _(dve):
            def add_window(g, h):
                dve.wait_ge(group_done, g + 1)
                base = dve.value_load(d.base_i[0:1, bass.ds(g, 1)], min_val=0, max_val=N)
                if not isinstance(g, int) or g > 0:
                    dve.wait_ge(window_added, g)
                at = bass.ds(base, P)
                nc.vector.tensor_tensor(d.attr_sums[:, at], d.attr_sums[:, at], win_bank[h][:, 0:P], ALU.add).then_inc(window_added, 1)

            def half(i, h, first):
                g = 2 * i + h
                dve.wait_ge(rec_in[h], 16 * (i + 1))
                if not first:
                    dve.wait_ge(group_done, g - 1)
                per_edge = lambda r: rec[:, h, r, :].unsqueeze(2).to_broadcast([P, J, P])
                by_chunk = lambda t: t[:, h, :, :].rearrange("p q j -> p j q")
                if windowed:
                    dve.wait_ge(rel_in[h], 16 * (i + 1))
                    nc.vector.tensor_scalar(spread_hot[:, h, :, :], by_chunk(rel_b), d.part[:, 0:1], None, ALU.is_equal).then_inc(spread_ready, 1)
                dve.wait_ge(key_in[h], 16 * (i + 1))
                nc.vector.tensor_tensor(same[:, h, :, :], by_chunk(key_b), per_edge(key_row), ALU.is_equal).then_inc(same_ready, 1)
                if windowed:
                    nc.vector.tensor_tensor(sum_hot[:, h, :, :], d.iota[:].unsqueeze(1).to_broadcast([P, J, P]), per_edge(2),
                                            ALU.is_equal).then_inc(sum_ready, 1)
                dve.wait_ge(same_ready, g + 1)
                nc.vector.tensor_tensor(earlier[:], same[:, h, :, :], d.before_me[:].unsqueeze(1).to_broadcast([P, J, P]), ALU.mult).then_inc(step, 1)
                nc.vector.tensor_tensor(to_f[:], d.spare[:], rec[:, h, key_row, :], ALU.subtract)
                dve.wait_ge(step, 5 * g + 1)
                nc.vector.reduce_sum(before[:], earlier[:], AX_X).then_inc(step, 1)
                dve.wait_ge(step, 5 * g + 2)
                nc.vector.tensor_scalar(before[:], before[:], 0.0, None, ALU.is_gt).then_inc(step, 1)
                dve.wait_ge(step, 5 * g + 3)
                nc.vector.tensor_tensor(to_f[:], to_f[:], before[:], ALU.mult).then_inc(step, 1)
                dve.wait_ge(step, 5 * g + 4)
                nc.vector.tensor_tensor(to_f[:], to_f[:], rec[:, h, key_row, :], ALU.add).then_inc(step, 1)
                dve.wait_ge(step, 5 * g + 5)
                if not first:
                    for k in range(K):
                        dve.wait_ge(added[k], 16 * per_table * (g - 1))
                nc.vector.tensor_copy(to_i[:, h, :], to_f[:]).then_inc(to_ready, 1)
                dve.wait_ge(to_ready, g + 1)
                if windowed and not (first and h == 0):
                    add_window(g - 1, 1 - h)

            loop(dve, half)
            if windowed:
                add_window(NG - 1, 1)

        @block.tensor
        def _(pe):
            def half(i, h, first):
                g = 2 * i + h

                def spread(j):
                    if not windowed or j >= J:
                        return
                    if not (first and h == 0 and j < 2):
                        pe.wait_ge(paid, J * g + j - 1)
                    nc.tensor.matmul(row_bank[j % 2][:, 0:F], spread_hot[:, h, j, :], window[:, h, :], start=True, stop=True).then_inc(row_ready, 1)

                if windowed:
                    pe.wait_ge(spread_ready, g + 1)
                    pe.wait_ge(window_in[h], 16 * (i + 1))
                spread(0)
                spread(1)
                pe.wait_ge(same_ready, g + 1)
                if windowed:
                    pe.wait_ge(sum_ready, g + 1)
                    if not first:
                        pe.wait_ge(window_added, g - 1)
                if attr:
                    pe.wait_ge(attr_in[h], 16 * (i + 1))
                    if isinstance(i, int) and g == FULL:
                        pe.wait_ge(tail_in, 16)
                for j in range(J):
                    ends = dict(start=(j == 0), stop=(j == J - 1))
                    if window_sums:
                        nc.tensor.matmul(win_bank[h][:, 0:P], attrs[:, h, j, :], sum_hot[:, h, j, :], **ends)
                    pe.wait_ge(paid, J * g + j + 1)
                    if not (first and h == 0 and j < B):
                        pe.wait_ge(staged, J * g + j + 1 - B)
                    last = nc.tensor.matmul(bank[j % B][:, 0:F], same[:, h, j, :], pay[:, h, j, :], start=True, stop=True)
                    if attr:
                        last = nc.tensor.matmul(bank[j % B][:, F:2 * F], same[:, h, j, :], attrs[:, h, j, :], start=True, stop=True)
                    last.then_inc(summed, 1)
                    spread(j + 2)
                pe.wait_ge(summed, J * (g + 1))
                pe.sem_inc(group_done, 1)

            loop(pe, half)

        @block.scalar
        def _(act):
            def half(i, h, first):
                g = 2 * i + h

                def make_pay(j):
                    if j >= J:
                        return
                    if j == 0:
                        act.wait_ge(rec_in[h], 16 * (i + 1))
                        if not first:
                            act.wait_ge(group_done, g - 1)
                    if windowed:
                        act.wait_ge(row_ready, J * g + j + 1)
                        row = row_bank[j % 2][:, 0:F]
                    else:
                        act.wait_ge(rows_in[h][j], 16 * (i + 1))
                        row = rows[:, h, j, :]
                    if weighted:
                        nc.scalar.activation(pay[:, h, j, :], row, ACT.Copy, scale=rec[:, h, 3, j:j + 1]).then_inc(paid, 1)
                    else:
                        nc.scalar.copy(pay[:, h, j, :], row).then_inc(paid, 1)

                make_pay(0)
                for j in range(J):
                    make_pay(j + 1)
                    act.wait_ge(summed, J * g + j + 1)
                    if not first:
                        act.wait_ge(added[j % K], 16 * (per_table * (g - 2) + j // K + 1))
                    nc.scalar.copy(sums[:, h, j, :], bank[j % B][:, 0:width]).then_inc(staged, 1)

            loop(act, half)


def gcn_nodes(nc, d):
    with ExitStack() as ctx:
        sb = lambda name, shape, dt=F32: ctx.enter_context(nc.sbuf_tensor("n1_" + name, shape, dt))
        sem = semaphores(nc, ctx, "n1_")
        HT = NT // 2
        PB = 3
        acc = sb("acc", [NP, NT, F])
        part = sb("part", [NP, PB, HT, F])
        x = sb("x", [NP, NT, F])
        scaled = sb("scaled", [NP, 2, F])
        accT = sb("accT", [F, 2, NP])
        squares = sb("squares", [NP, 2, F])
        w = sb("w", [F, F])
        bias = sb("bias", [NP, F])
        stat = sb("stat", [NP, 3, NT])
        EC = E // NP
        one = sb("one", [NP, EC])
        next_one = sb("next_one", [NP, EC])
        cnt_tp = sb("cnt_tp", [TILES, P])
        cnt_pt = sb("cnt_pt", [P, TILES])
        tile_cnt = sb("tile_cnt", [TILES, 1])
        tile_cnt_b = sb("tile_cnt_b", [TILES, P])
        after_me = sb("after_me", [P, P])
        start = sb("start", [P, TILES])
        near_row = sb("near_row", [P, TILES])
        near_row_i = sb("near_row_i", [P, TILES], I32)
        first_at = sb("first_at", [P, TILES])
        end_at = sb("end_at", [P, TILES])
        bad = sb("bad", [P, 2])
        near = sb("near", [P, TILES, SLOTS])
        hi = sb("hi", [P, TILES, SLOTS])
        outside = sb("outside", [P, TILES, SLOTS])
        outside2 = sb("outside2", [P, TILES, SLOTS])
        place_bank, prod, small = d.bank[0:4], d.bank[5:7], d.bank[7]
        turned = (d.bank[4], d.bank[7])
        turned_at = lambda t: turned[t % 2][:, 0:NP]
        cnt_turn, start_bank, bad_sum = small[:, 0:TILES], small[:, P:P + TILES], small[0:1, 2 * P:2 * P + 1]
        batches = [(t, min(t + 4, SUPER)) for t in range(0, SUPER, 4)]
        acc_in = [sem(f"acc_in{r}") for r in range(2)]
        part_in = [sem(f"part_in{b}") for b in range(PB)]
        x_in, w_in, part_used, done = sem("x_in"), sem("w_in"), sem("part_used"), sem("done")
        turn_ready, accT_ready, prod_ready, prod_used = sem("turn_ready"), sem("accT_ready"), sem("prod_ready"), sem("prod_used")
        x1_ready, mean_ready, squared, var_ready = sem("x1_ready"), sem("mean_ready"), sem("squared"), sem("var_ready")
        std_ready, scale_ready, h_ready, stored = sem("std_ready"), sem("scale_ready"), sem("h_ready"), sem("stored")
        cnt_stored, cnt_in, dst_in = sem("cnt_stored"), sem("cnt_in"), sem("dst_in")
        zeroed, cnt_ready, cnt_turned, cnt_copied = sem("zeroed"), sem("cnt_ready"), sem("cnt_turned"), sem("cnt_copied")
        start_ready, row_ready, bad_ready, bad_summed = sem("start_ready"), sem("row_ready"), sem("bad_ready"), sem("bad_summed")
        turns, near_in, places_ready = sem("turns"), sem("near_in"), sem("places_ready")
        places_turned, places_copied = sem("places_turned"), sem("places_copied")
        block = ctx.enter_context(nc.Block())
        nodes = lambda t: t[0:N, :].rearrange("(p t) f -> p t f", p=NP)
        half = lambda t, r: t[:, r * HT:(r + 1) * HT, :]

        @block.sync
        def _(sp):
            def load_part(n):
                r, k = divmod(n, K)
                if n >= PB:
                    sp.wait_ge(part_used, n - PB + 1)
                sp.dma_start(part[:, n % PB, :, :], half(nodes(d.tab_gcn[k]), r)[:, :, 0:F]).then_inc(part_in[n % PB], 16)

            sp.dma_start(d.count_dst.rearrange("(p t) -> p t", p=NP), d.cnt_dst[:]).then_inc(cnt_stored, 16)
            for at, t in ((0, one), (1, next_one)):
                sp.dma_start(t[:], d.dst_f[at:at + E].rearrange("(p c) -> p c", p=NP)).then_inc(dst_in, 16)
            sp.dma_start(half(acc, 0), half(nodes(d.g), 0)).then_inc(acc_in[0], 16)
            for n in range(PB):
                load_part(n)
            sp.wait_ge(cnt_stored, 16)
            sp.wait_ge(zeroed, 1)
            whole, rest = divmod(N, P)
            sp.dma_start(cnt_tp[0:whole, :], d.count_dst[0:whole * P].rearrange("(t p) -> t p", p=P)).then_inc(cnt_in, 16)
            sp.dma_start(cnt_tp[whole:whole + 1, 0:rest], d.count_dst[whole * P:N].rearrange("(t p) -> t p", t=1)).then_inc(cnt_in, 16)
            for n in range(PB, K):
                load_part(n)
            sp.dma_start(w[:], d.kernel).then_inc(w_in, 16)
            sp.dma_start(bias[:], d.bias.rearrange("(o f) -> o f", o=1).to_broadcast([NP, F])).then_inc(w_in, 16)
            sp.dma_start(x[:], nodes(d.x)).then_inc(x_in, 16)
            sp.dma_start(half(acc, 1), half(nodes(d.g), 1)).then_inc(acc_in[1], 16)
            for n in range(K, 2 * K):
                load_part(n)
            sp.dma_start(d.attr_t, d.attr_sums[:]).then_inc(stored, 16)
            sp.wait_ge(x1_ready, NT)
            sp.dma_start(nodes(d.x1), x[:]).then_inc(stored, 16)
            for r in range(2):
                sp.wait_ge(h_ready, HT * (r + 1))
                sp.dma_start(half(nodes(d.h1), r), half(acc, r)).then_inc(stored, 16)
            sp.wait_ge(stored, 16 * 4)

        @block.gpsimd
        def _(pool):
            pool.wait_ge(row_ready, 1)
            pool.sem_inc(turns, 1)
            for t in range(TILES):
                nc.gpsimd.indirect_dma_start(
                    out=near[:, t, :], out_offset=None, in_=d.near,
                    in_offset=bass.IndirectOffsetOnAxis(ap=near_row_i[:, t:t + 1], axis=0)).then_inc(near_in, 16)

        @block.vector
        def _(dve):
            count = [0]

            def link(ins):
                count[0] += 1
                ins.then_inc(done, 1)
                dve.wait_ge(done, count[0])

            def starts():
                nc.vector.memset(cnt_tp[:], 0.0).then_inc(zeroed, 1)
                nc.vector.memset(bad[:], 0.0)
                nc.vector.tensor_scalar(after_me[:], d.iota[:], d.part[:, 0:1], None, ALU.is_gt)
                dve.wait_ge(dst_in, 32)
                link(nc.vector.tensor_tensor(one[:], next_one[:], one[:], ALU.subtract))
                link(nc.vector.tensor_reduce(bad[0:NP, 0:1], one[:], AX_X, ALU.min))
                link(nc.vector.tensor_scalar(bad[0:NP, 0:1], bad[0:NP, 0:1], -0.5, None, ALU.is_lt))
                dve.wait_ge(cnt_in, 32)
                link(nc.vector.reduce_sum(tile_cnt[:], cnt_tp[:], AX_X))
                nc.vector.tensor_copy(tile_cnt_b[:], tile_cnt[:].to_broadcast([TILES, P])).then_inc(cnt_ready, 1)
                dve.wait_ge(cnt_turned, 1)
                nc.vector.tensor_copy(cnt_pt[:], cnt_turn).then_inc(cnt_copied, 1)
                dve.wait_ge(cnt_copied, 1)
                dve.wait_ge(start_ready, 1)
                link(nc.vector.tensor_copy(start[:], start_bank))
                link(nc.vector.tensor_scalar(near_row[:], start[:], 1.0 / STEP, 0.5 / STEP - 0.5, ALU.mult, ALU.add))
                link(nc.vector.tensor_scalar(near_row[:], near_row[:], ROUND, ROUND, ALU.add, ALU.subtract))
                nc.vector.tensor_copy(near_row_i[:], near_row[:]).then_inc(row_ready, 1)
                link(nc.vector.scalar_tensor_tensor(first_at[:], near_row[:], -float(STEP), start[:], ALU.mult, ALU.add))
                link(nc.vector.tensor_tensor(end_at[:], first_at[:], cnt_pt[:], ALU.add))
                link(nc.vector.tensor_reduce(bad[:, 1:2], end_at[:], AX_X, ALU.max))
                link(nc.vector.tensor_scalar(bad[:, 1:2], bad[:, 1:2], SLOTS + 0.5, None, ALU.is_gt))
                nc.vector.tensor_tensor(bad[:, 0:1], bad[:, 0:1], bad[:, 1:2], ALU.max).then_inc(bad_ready, 1)
                dve.wait_ge(bad_summed, 1)
                link(nc.vector.tensor_copy(stat[0:1, 0, 0:1], d.windowed[:]))
                link(nc.vector.tensor_scalar(stat[0:1, 1, 0:1], bad_sum, 0.5, None, ALU.is_lt))
                link(nc.vector.tensor_tensor(stat[0:1, 0, 0:1], stat[0:1, 0, 0:1], stat[0:1, 1, 0:1], ALU.mult))
                link(nc.vector.tensor_copy(d.dense[:], stat[0:1, 0, 0:1]))

            def places():
                place = d.iota[:, 0:SLOTS].unsqueeze(1).to_broadcast([P, TILES, SLOTS])
                per_node = lambda t: t[:].unsqueeze(2).to_broadcast([P, TILES, SLOTS])
                nc.vector.tensor_tensor(outside[:], place, per_node(first_at), ALU.is_lt)
                link(nc.vector.tensor_tensor(outside2[:], place, per_node(end_at), ALU.is_ge))
                link(nc.vector.tensor_tensor(outside[:], outside[:], outside2[:], ALU.add))
                dve.wait_ge(near_in, 16 * TILES)
                link(nc.vector.tensor_scalar(hi[:], near[:], 1.0 / P, 0.5 / P - 0.5, ALU.mult, ALU.add))
                link(nc.vector.tensor_scalar(hi[:], hi[:], ROUND, ROUND, ALU.add, ALU.subtract))
                nc.vector.scalar_tensor_tensor(near[:], hi[:], -float(P), near[:], ALU.mult, ALU.add)
                link(nc.vector.scalar_tensor_tensor(outside[:], outside[:], float(P // 2), hi[:], ALU.mult, ALU.add))
                for b in range(2):
                    last = nc.vector.tensor_scalar(hi[:, b:TILES:2, :], outside[:, b:TILES:2, :], 2.0, float(b), ALU.mult, ALU.add)
                    last.then_inc(places_ready, 1)

            def add_up(r):
                dve.wait_ge(acc_in[r], 16)
                for n in range(r * K, (r + 1) * K):
                    dve.wait_ge(part_in[n % PB], 16 * (n // PB + 1))
                    nc.vector.tensor_tensor(half(acc, r), half(acc, r), part[:, n % PB, :, :], ALU.add).then_inc(part_used, 1)
                    dve.wait_ge(part_used, n + 1)

            def products(r):
                for t in range(r * HT, (r + 1) * HT):
                    dve.wait_ge(prod_ready, t + 1)
                    nc.vector.scalar_tensor_tensor(scaled[:, t % 2, :], prod[t % 2][0:NP, 0:F], d.dinv[:, t:t + 1], bias[:],
                                                   ALU.mult, ALU.add).then_inc(prod_used, 1)
                    dve.wait_ge(prod_used, t + 1)
                    nc.vector.scalar_tensor_tensor(x[:, t, :], scaled[:, t % 2, :], 0.0, x[:, t, :], ALU.max, ALU.add,
                                                   accum_out=stat[:, 0, t:t + 1]).then_inc(x1_ready, 1)
                dve.wait_ge(x1_ready, HT * (r + 1))
                here = slice(r * HT, (r + 1) * HT)
                nc.vector.tensor_scalar(stat[:, 0, here], stat[:, 0, here], -1.0 / F, None, ALU.mult).then_inc(mean_ready, 1)

            starts()
            add_up(0)
            dve.wait_ge(w_in, 32)
            dve.wait_ge(x_in, 16)
            products(0)
            places()
            add_up(1)
            products(1)
            dve.wait_ge(squared, NT)
            nc.vector.tensor_scalar(stat[:, 1, :], stat[:, 1, :], 1.0 / F, LN_EPS, ALU.mult, ALU.add).then_inc(var_ready, 1)
            dve.wait_ge(std_ready, 1)
            link(nc.vector.reciprocal(stat[:, 1, :], stat[:, 2, :]))
            dve.wait_ge(mean_ready, 2)
            nc.vector.tensor_tensor(stat[:, 0, :], stat[:, 0, :], stat[:, 1, :], ALU.mult).then_inc(scale_ready, 1)

        @block.tensor
        def _(pe):
            pe.wait_ge(cnt_ready, 1)
            nc.tensor.transpose(cnt_turn, cnt_tp[:], d.ident[0:TILES, 0:TILES]).then_inc(cnt_turned, 1)
            pe.wait_ge(cnt_copied, 1)
            nc.tensor.matmul(start_bank, after_me[:], cnt_pt[:], start=True, stop=False)
            nc.tensor.matmul(start_bank, tile_cnt_b[:], after_me[0:TILES, 0:TILES], start=False, stop=True).then_inc(start_ready, 1)
            pe.wait_ge(bad_ready, 1)
            nc.tensor.matmul(bad_sum, bad[:, 0:1], d.ones[:, 0:1], start=True, stop=True).then_inc(bad_summed, 1)

            def turn(t):
                if t >= 2:
                    pe.wait_ge(accT_ready, t - 1)
                nc.tensor.transpose(turned_at(t), acc[:, t, :], d.ident[0:NP, 0:NP]).then_inc(turn_ready, 1)

            def tiles(r):
                pe.wait_ge(part_used, K * (r + 1))
                turn(r * HT)
                for t in range(r * HT, (r + 1) * HT):
                    if t + 1 < (r + 1) * HT:
                        turn(t + 1)
                    if t >= 2:
                        pe.wait_ge(prod_used, t - 1)
                    pe.wait_ge(accT_ready, t + 1)
                    nc.tensor.matmul(prod[t % 2][0:NP, 0:F], accT[:, t % 2, :], w[:], start=True, stop=True).then_inc(prod_ready, 1)

            pe.wait_ge(w_in, 32)
            tiles(0)
            pe.wait_ge(places_ready, 2)
            for n, (t0, t1) in enumerate(batches):
                for m, what in enumerate((near, hi)):
                    if n >= 2:
                        pe.wait_ge(places_copied, 2 * (n - 2) + m + 1)
                    for t in range(t0, t1):
                        last = nc.tensor.transpose(place_bank[2 * m + n % 2][:, (t - t0) * P:(t - t0 + 1) * P],
                                                   what[:, 2 * t:2 * t + 2, :].rearrange("p b s -> p (b s)"), d.ident[:])
                    last.then_inc(places_turned, 1)
            tiles(1)

        @block.scalar
        def _(act):
            def turns_of(r):
                for t in range(r * HT, (r + 1) * HT):
                    act.wait_ge(turn_ready, t + 1)
                    if t >= 2:
                        act.wait_ge(prod_ready, t - 1)
                    nc.scalar.copy(accT[:, t % 2, :], turned_at(t)).then_inc(accT_ready, 1)

            def square(r):
                act.wait_ge(mean_ready, r + 1)
                for t in range(r * HT, (r + 1) * HT):
                    if t >= 2:
                        act.wait_ge(squared, t - 1)
                    nc.scalar.activation(squares[:, t % 2, :], x[:, t, :], ACT.Square, bias=stat[:, 0, t:t + 1],
                                         accum_out=stat[:, 1, t:t + 1]).then_inc(squared, 1)

            turns_of(0)
            for n, (t0, t1) in enumerate(batches):
                for m, kept in enumerate((d.lo, d.hi)):
                    act.wait_ge(places_turned, 2 * n + m + 1)
                    nc.scalar.copy(kept[:, t0:t1, :].rearrange("p t q -> p (t q)"), place_bank[2 * m + n % 2][:, 0:(t1 - t0) * P]).then_inc(places_copied, 1)
            square(0)
            turns_of(1)
            square(1)
            act.wait_ge(var_ready, 1)
            nc.scalar.activation(stat[:, 2, :], stat[:, 1, :], ACT.Sqrt).then_inc(std_ready, 1)
            act.wait_ge(scale_ready, 1)
            for t in range(NT):
                nc.scalar.activation(acc[:, t, :], x[:, t, :], ACT.Relu, bias=stat[:, 0, t:t + 1], scale=stat[:, 1, t:t + 1]).then_inc(h_ready, 1)


def dense_sums(nc, d):
    with ExitStack() as ctx:
        sb = lambda nm, shape, dt=F32: ctx.enter_context(nc.sbuf_tensor("ds_" + nm, shape, dt))
        sem = semaphores(nc, ctx, "ds_")
        QN = WJ
        GOES = PAIRS // QN
        PB = 4
        BATCHES = PAIRS // PB
        PER_GO = QN // PB
        HB = 4
        BLOCKS = -(-HI // HB)
        CHUNK = 10
        CHUNKS = TILES // CHUNK
        POOL_CHUNKS = 2
        src_sums = d.src_sums
        parts = sb("parts", [P, TILES, 3, F], BF16)
        now = sb("now", [P, 2, 2, 3, F], BF16)
        counts = sb("counts", [P, 2, HI, 2, P], BF16)
        turned = sb("turned", [P, 2, 2, HB * P], BF16)
        lo_hot = sb("lo_hot", [P, 2, P, QN], BF16)
        hi_hot = sb("hi_hot", [P, 2, HH, QN], BF16)
        numbers = sb("numbers", [P, P, QN], BF16)
        ident_b = sb("ident_b", [P, P], BF16)
        row_stage = sb("row_stage", [F, 2, 2 * P])
        pair_bank, row_bank, back_bank = d.bank[0:3], d.bank[3], d.bank[6:8]
        B = len(pair_bank)
        turn_bank = [b[:].bitcast(BF16) for b in d.bank[4:6]]
        h1_in = [sem(f"h1_in{c}") for c in range(CHUNKS)]
        parts_ready = [sem(f"parts_ready{c}") for c in range(CHUNKS)]
        ready, done, cut, src_zeroed = sem("ready"), sem("done"), sem("cut"), sem("src_zeroed")
        hot_ready = sem("hot_ready")
        pair_ready, pair_copied = sem("pair_ready"), sem("pair_copied")
        turn_ready, turn_copied = sem("turn_ready"), sem("turn_copied")
        back_ready, src_added = sem("back_ready"), sem("src_added")
        row_ready, row_copied = sem("row_ready"), sem("row_copied")
        row_stored = [sem(f"row_stored{h}") for h in range(2)]
        now_ready, store_turns = sem("now_ready"), sem("store_turns")
        acc_in, part_in = ([sem(f"{nm}{h}") for h in range(2)] for nm in ("acc_in", "part_in"))
        part_used, attr_in = sem("part_used"), sem("attr_in")
        block = ctx.enter_context(nc.Block())
        FIRST_GO = {1: 2, 2: 3, 4: 4, 5: 5, 6: 6, 8: 7}
        AHEAD_GO = {10: 0, 11: 1}
        wide = lambda b: min(HB, HI - b * HB)

        def cut_chunk(eng, ops, c, link):
            tiles = slice(c * CHUNK, (c + 1) * CHUNK)
            h1 = src_sums[:, c * CHUNK * F:(c + 1) * CHUNK * F].rearrange("p (t f) -> p t f", f=F)
            eng.wait_ge(h1_in[c], 16)
            link(ops.tensor_copy(parts[:, tiles, 0, :], h1))
            link(ops.tensor_tensor(h1, h1, parts[:, tiles, 0, :], ALU.subtract))
            link(ops.tensor_copy(parts[:, tiles, 1, :], h1))
            ops.tensor_tensor(parts[:, tiles, 2, :], h1, parts[:, tiles, 1, :], ALU.subtract).then_inc(parts_ready[c], 1)
            eng.wait_ge(parts_ready[c], 1)
            ops.memset(src_sums[:, c * CHUNK * F:(c + 1) * CHUNK * F], 0.0).then_inc(src_zeroed, 1)

        def loop(eng, pair_of_tiles, head=1, peeled=0):
            for i in range(head):
                pair_of_tiles(i, 0, i == 0, False)
                pair_of_tiles(i, 1, i == 0, False)
            last = SUPER // 2 - peeled
            with eng.Fori(head, last) as i:
                pair_of_tiles(i, 0, False, False)
                pair_of_tiles(i, 1, False, False)
            for i in range(last, SUPER // 2):
                pair_of_tiles(i, 0, False, False)
                pair_of_tiles(i, 1, False, False)
            pair_of_tiles(SUPER // 2, 0, False, True)

        @block.sync
        def _(sp):
            for c in range(CHUNKS):
                tiles = slice(c * CHUNK, (c + 1) * CHUNK)
                sp.dma_start(src_sums[:].rearrange("p (t f) -> p t f", f=F)[:, tiles, :],
                             d.h1.rearrange("(t p) f -> p t f", p=P)[:, tiles, :]).then_inc(h1_in[c], 16)

            def store(i, h, first, last):
                t = 2 * i + h
                if isinstance(i, int) and i == 0:
                    sp.dma_start(d.src_attr_half(h), d.table_half(0, h)).then_inc(acc_in[h], 16)
                elif isinstance(i, int) and i < K:
                    if i >= 2:
                        sp.wait_ge(part_used, 2 * (i - 2) + h + 1)
                    sp.dma_start(d.part_half(h), d.table_half(i, h)).then_inc(part_in[h], 16)
                elif isinstance(i, int) and i == K and h == 0:
                    sp.wait_ge(part_used, 2 * (K - 1))
                    sp.dma_start(d.attr_by_dst[:, 0:N], d.attr_t[:, 0:N]).then_inc(attr_in, 16)
                sp.wait_ge(row_copied, t + 1)
                sp.sem_inc(store_turns, 1)
                sp.dma_start(d.row_t[:, bass.ds(t * 2 * P, 2 * P)], row_stage[:, h, :]).then_inc(row_stored[h], 16)

            loop(sp, store, head=K + 1)
            sp.wait_ge(attr_in, 16)
            for h in range(2):
                sp.wait_ge(row_stored[h], 16 * ((SUPER + 1 - h) // 2))

        @block.gpsimd
        def _(pool):
            count = [0]

            def link(ins):
                count[0] += 1
                ins.then_inc(cut, 1)
                pool.wait_ge(cut, count[0])

            cut_chunk(pool, nc.gpsimd, 0, link)

            def take(i, h, first, last):
                t = 2 * i + h
                if isinstance(i, int) and i == 0 and h == 1:
                    for c in range(1, POOL_CHUNKS):
                        cut_chunk(pool, nc.gpsimd, c, link)
                if isinstance(i, int) and i == 1 and h == 0:
                    for c in range(POOL_CHUNKS, CHUNKS):
                        pool.wait_ge(parts_ready[c], 1)
                if not first:
                    pool.wait_ge(back_ready, BLOCKS * (t - 1))
                nc.gpsimd.tensor_copy(now[:, h, :, :, :], parts[:, bass.ds(2 * t, 2), :, :]).then_inc(now_ready, 1)
                if isinstance(i, int) and 1 <= i < K:
                    pool.wait_ge(acc_in[h], 16)
                    pool.wait_ge(part_in[h], 16 * i)
                    if i >= 2:
                        pool.wait_ge(part_used, 2 * (i - 2) + h + 1)
                    nc.gpsimd.tensor_tensor(d.src_attr_half(h), d.src_attr_half(h), d.part_half(h), ALU.add).then_inc(part_used, 1)

            loop(pool, take, head=K)

        @block.vector
        def _(dve):
            count = [0]

            def link(ins):
                count[0] += 1
                ins.then_inc(done, 1)
                dve.wait_ge(done, count[0])

            def one_hots(t, go, first=False):
                if not (first and go < 2):
                    dve.wait_ge(pair_ready, BATCHES * t + PER_GO * (go - 1))
                per_place = lambda a, n: a[:, bass.ds(t, 1), go * QN:(go + 1) * QN].to_broadcast([P, n, QN])
                nc.vector.tensor_tensor(lo_hot[:, go % 2, :, :], numbers[:], per_place(d.lo, P), ALU.is_equal)
                nc.vector.tensor_tensor(hi_hot[:, go % 2, :, :], numbers[:, 0:HH, :], per_place(d.hi, HH), ALU.is_equal).then_inc(hot_ready, 1)

            nc.vector.tensor_copy(ident_b[:], d.ident[:]).then_inc(ready, 1)
            link(nc.vector.tensor_copy(numbers[:], d.iota[:].unsqueeze(2).to_broadcast([P, P, QN])))
            for go in range(GOES):
                one_hots(0, go, first=True)
            for c in range(POOL_CHUNKS, CHUNKS):
                cut_chunk(dve, nc.vector, c, link)
            one_hots(1, 0)
            one_hots(1, 1)
            dve.wait_ge(src_zeroed, CHUNKS)

            def add(i, h, first, last):
                t = 2 * i + h
                for b in range(BLOCKS):
                    if b in FIRST_GO and not last:
                        one_hots(t + 1, FIRST_GO[b])
                    if b in AHEAD_GO and not (isinstance(i, int) and t + 2 >= SUPER):
                        one_hots(t + 2, AHEAD_GO[b])
                    u = BLOCKS * t + b
                    n = wide(b) * P
                    here = src_sums[:, b * HB * P:b * HB * P + n]
                    dve.wait_ge(back_ready, u + 1)
                    if not (first and h == 0):
                        dve.wait_ge(src_added, u - BLOCKS + 1)
                    nc.vector.tensor_tensor(here, here, back_bank[(BLOCKS * h + b) % 2][:, 0:n], ALU.add).then_inc(src_added, 1)

            loop(dve, add, peeled=1)

        @block.tensor
        def _(pe):
            def pairs(t, h, batch, first=False):
                go, at = divmod(batch, PER_GO)
                if at == 0:
                    pe.wait_ge(hot_ready, GOES * t + go + 1)
                if not (first and batch < B):
                    back = B if batch >= B else batch + BATCHES - max(n for n in range(BATCHES) if n % B == batch)
                    pe.wait_ge(pair_copied, BATCHES * t + batch - back + 1)
                for c in range(PB):
                    q = at * PB + c
                    last = nc.tensor.matmul(pair_bank[batch % B][:, c * HH:(c + 1) * HH], lo_hot[:, go % 2, :, q], hi_hot[:, go % 2, :, q],
                                            start=True, stop=True)
                last.then_inc(pair_ready, 1)

            pe.wait_ge(ready, 1)
            for batch in range(BATCHES):
                pairs(0, 0, batch, first=True)
            def products(i, h, first, last):
                t = 2 * i + h
                pe.wait_ge(pair_copied, BATCHES * (t + 1))

                def turn(b):
                    if b >= BLOCKS:
                        return
                    u, v = BLOCKS * t + b, (BLOCKS * h + b) % 2
                    if not (first and h == 0 and b < 2):
                        pe.wait_ge(turn_copied, u - 1)
                    for half in range(2):
                        for k in range(wide(b)):
                            at = (half * HB + k) * P
                            ins = nc.tensor.transpose(turn_bank[v][:, at:at + P], counts[:, h, b * HB + k, half, :], ident_b[:])
                    ins.then_inc(turn_ready, 1)

                turn(0)
                for b in range(BLOCKS):
                    turn(b + 1)
                    ahead = [] if last else list(range(3 * b, min(3 * b + 3, BATCHES)))
                    for k in range(wide(b)):
                        tile = b * HB + k
                        if tile == 0 and not (first and h == 0):
                            pe.wait_ge(row_copied, t)
                        if first and h == 0 and tile % CHUNK == 0:
                            pe.wait_ge(parts_ready[tile // CHUNK], 1)
                        for s in range(3):
                            ins = nc.tensor.matmul(row_bank[:, 0:2 * P], parts[:, tile, s, :],
                                                   counts[:, h, tile, :, :].rearrange("p b q -> p (b q)"),
                                                   start=(tile == 0 and s == 0), stop=(tile == HI - 1 and s == 2))
                        if ahead:
                            pairs(t + 1, 1 - h, ahead.pop(0))
                    if b == BLOCKS - 1:
                        ins.then_inc(row_ready, 1)
                    u, v = BLOCKS * t + b, (BLOCKS * h + b) % 2
                    if b == 0:
                        pe.wait_ge(now_ready, t + 1)
                    pe.wait_ge(turn_copied, u + 1)
                    if not (first and h == 0 and b < 2):
                        pe.wait_ge(src_added, u - 1)
                    n = wide(b) * P
                    for half in range(2):
                        for s in range(3):
                            ins = nc.tensor.matmul(back_bank[v][:, 0:n], now[:, h, half, s, :], turned[:, v, half, 0:n],
                                                   start=(half == 0 and s == 0), stop=(half == 1 and s == 2))
                    ins.then_inc(back_ready, 1)

            loop(pe, products)

        @block.scalar
        def _(act):
            def keep_counts(t, h, batch, first=False):
                if batch == 0 and not first:
                    act.wait_ge(back_ready, BLOCKS * (t - 1))
                act.wait_ge(pair_ready, BATCHES * t + batch + 1)
                to = counts[:, h, :, :, :].rearrange("p t b q -> p (t b) q")[:, :, batch * PB:(batch + 1) * PB]
                nc.scalar.copy(to, pair_bank[batch % B][:, 0:PB * HH].rearrange("p (c k) -> p k c", c=PB)).then_inc(pair_copied, 1)

            for batch in range(BATCHES):
                keep_counts(0, 0, batch, first=True)

            def copies(i, h, first, last):
                t = 2 * i + h

                def keep_turned(b):
                    if b >= BLOCKS:
                        return
                    u, v = BLOCKS * t + b, (BLOCKS * h + b) % 2
                    act.wait_ge(turn_ready, u + 1)
                    if not (first and h == 0 and b < 2):
                        act.wait_ge(back_ready, u - 1)
                    n = wide(b) * P
                    nc.scalar.copy(turned[:, v, :, 0:n], turn_bank[v].rearrange("p (b q) -> p b q", b=2)[:, :, 0:n]).then_inc(turn_copied, 1)

                keep_turned(0)
                for b in range(BLOCKS):
                    keep_turned(b + 1)
                    if not last:
                        for batch in range(3 * b, min(3 * b + 3, BATCHES)):
                            keep_counts(t + 1, 1 - h, batch, first=(first and h == 0))
                act.wait_ge(row_ready, t + 1)
                if not first:
                    act.wait_ge(row_stored[h], 16 * i)
                nc.scalar.copy(row_stage[:, h, :], row_bank[:, 0:2 * P]).then_inc(row_copied, 1)

            loop(act, copies)


def clear_tables(nc, tables):
    with ExitStack() as ctx:
        sem = semaphores(nc, ctx, "clear_")
        zeroed, cleared = sem("zeroed"), sem("cleared")
        CUT = 5
        zeros = ctx.enter_context(nc.sbuf_tensor("clear_zeros", [P, ROWS // P // CUT * 2 * F], F32))
        block = ctx.enter_context(nc.Block())

        @block.gpsimd
        def _(pool):
            nc.gpsimd.memset(zeros[:], 0.0).then_inc(zeroed, 1)

        @block.sync
        def _(sp):
            sp.wait_ge(zeroed, 1)
            for t in tables:
                view = t.rearrange("(p q r) c -> p q (r c)", p=P, q=CUT)
                for q in range(CUT):
                    sp.dma_start(view[:, q, :], zeros[:, 0:view.shape[2]]).then_inc(cleared, 16)
            sp.wait_ge(cleared, 16 * CUT * len(tables))


def turn_tables(nc, d, name, tables, outs):
    with ExitStack() as ctx:
        sb = lambda nm, shape, dt=F32: ctx.enter_context(nc.sbuf_tensor(f"{name}_{nm}", shape, dt))
        sem = semaphores(nc, ctx, name + "_")
        M = len(outs)
        part = sb("part", [P, K, M * F])
        total = sb("total", [P, M * F])
        stage = sb("stage", [P, M, P])
        loaded, added, turned, folded, stored = sem("loaded"), sem("added"), sem("turned"), sem("folded"), sem("stored")
        store_turns = sem("store_turns")
        turn = d.bank[0:M]
        block = ctx.enter_context(nc.Block())

        @block.sync
        def _(sp):
            def block_of_rows(b):
                at = bass.ds(b * P, P)
                for k in range(K):
                    sp.dma_start(part[:, k, :], tables[k][at, 0:M * F]).then_inc(loaded, 16)
                sp.wait_ge(folded, M * (b + 1))
                sp.sem_inc(store_turns, 1)
                for m, out in enumerate(outs):
                    sp.dma_start(out[:, at], stage[:, m, :]).then_inc(stored, 16)

            block_of_rows(0)
            with sp.Fori(1, ROWS // P) as b:
                block_of_rows(b)
            sp.wait_ge(stored, 16 * M * (ROWS // P))

        @block.vector
        def _(dve):
            with dve.Fori(0, ROWS // P) as b:
                dve.wait_ge(loaded, 16 * K * (b + 1))
                nc.vector.reduce_sum(total[:], part[:].rearrange("p k f -> p f k"), AX_X).then_inc(added, 1)

        @block.tensor
        def _(pe):
            with pe.Fori(0, ROWS // P) as b:
                pe.wait_ge(added, b + 1)
                for m in range(M):
                    last = nc.tensor.transpose(turn[m][:, 0:P], total[:, m * F:(m + 1) * F], d.ident[:])
                last.then_inc(turned, 1)

        @block.scalar
        def _(act):
            def keep(b, first):
                act.wait_ge(turned, b + 1)
                if not first:
                    act.wait_ge(stored, 16 * M * b)
                for m in range(M):
                    nc.scalar.copy(stage[:, m, :], turn[m][:, 0:P]).then_inc(folded, 1)

            keep(0, True)
            with act.Fori(1, ROWS // P) as b:
                keep(b, False)


def load_sums(nc, d):
    with ExitStack() as ctx:
        sem = semaphores(nc, ctx, "load_")
        loaded, acc_in, part_used = sem("loaded"), sem("acc_in"), sem("part_used")
        part_in = [sem(f"part_in{h}") for h in range(2)]
        block = ctx.enter_context(nc.Block())

        @block.sync
        def _(sp):
            sp.dma_start(d.src_sums[:, 0:N], d.src_t[:, 0:N]).then_inc(loaded, 16)
            for h in range(2):
                sp.dma_start(d.src_attr_half(h), d.table_half(0, h)).then_inc(acc_in, 16)
            for k in range(1, K):
                for h in range(2):
                    if k >= 2:
                        sp.wait_ge(part_used, 2 * (k - 2) + h + 1)
                    sp.dma_start(d.part_half(h), d.table_half(k, h)).then_inc(part_in[h], 16)
            sp.wait_ge(part_used, 2 * (K - 1))
            sp.dma_start(d.attr_by_dst[:, 0:N], d.attr_t[:, 0:N]).then_inc(loaded, 16)
            sp.wait_ge(loaded, 32)

        @block.vector
        def _(dve):
            dve.wait_ge(acc_in, 32)
            for k in range(1, K):
                for h in range(2):
                    dve.wait_ge(part_in[h], 16 * k)
                    if k >= 2:
                        dve.wait_ge(part_used, 2 * (k - 2) + h + 1)
                    nc.vector.tensor_tensor(d.src_attr_half(h), d.src_attr_half(h), d.part_half(h), ALU.add).then_inc(part_used, 1)


def last_nodes(nc, d):
    with ExitStack() as ctx:
        sb = lambda name, shape, dt=F32: ctx.enter_context(nc.sbuf_tensor("n2_" + name, shape, dt))
        sem = semaphores(nc, ctx, "n2_")
        row_sums = sb("row_sums", [F, N])
        agg = sb("agg", [NP, NT, F])
        h1 = sb("h1", [NP, NT, F])
        x1 = sb("x1", [NP, NT, F])
        turn_sb = sb("turn_sb", [F, 2, NP])
        w = sb("w", [F, 4, F])
        per_feature = sb("per_feature", [NP, 4, F])
        biased = sb("biased", [NP, 2, F])
        leaky = sb("leaky", [NP, 2, F])
        squares = sb("squares", [NP, 2, F])
        stat = sb("stat", [NP, 3, NT])
        per_count = sb("per_count", [NP, NT])
        turned, prod = d.bank[0:2], d.bank[2:5]
        B = len(prod)
        HT = NT // 2
        SKEW = HT + 4
        w_in, row_in, h1_in, x1_in, done = sem("w_in"), sem("row_in"), sem("h1_in"), sem("x1_in"), sem("done")
        turn_ready, turn_copied = sem("turn_ready"), sem("turn_copied")
        prod_ready, prod_used = sem("prod_ready"), sem("prod_used")
        agg_ready, leaky_ready, sum_ready = sem("agg_ready"), sem("leaky_ready"), sem("sum_ready")
        mean_ready, squared, var_ready, std_ready = sem("mean_ready"), sem("squared"), sem("var_ready"), sem("std_ready")
        scale_ready, normed, beta_added = sem("scale_ready"), sem("normed"), sem("beta_added")
        scaled, out_ready, stored = sem("scaled"), sem("out_ready"), sem("stored")
        block = ctx.enter_context(nc.Block())
        nodes = lambda t: t[0:N, :].rearrange("(p t) f -> p t f", p=NP)
        half = lambda t, r: t[:, r * HT:(r + 1) * HT, :]

        @block.sync
        def _(sp):
            for m, a in enumerate((d.w_back[F:2 * F, :], d.w_back[0:F, :], d.w_fwd[F:2 * F, :], d.w_fwd[0:F, :])):
                sp.dma_start(w[:, m, :], a).then_inc(w_in, 16)
            for m, a in enumerate((d.b_back, d.b_fwd, d.gamma, d.beta)):
                sp.dma_start(per_feature[:, m, :], a.rearrange("(o f) -> o f", o=1).to_broadcast([NP, F])).then_inc(w_in, 16)
            sp.dma_start(row_sums[:], d.row_t[:, 0:N]).then_inc(row_in, 16)
            sp.dma_start(h1[:], nodes(d.h1)).then_inc(h1_in, 16)
            sp.dma_start(x1[:], nodes(d.x1)).then_inc(x1_in, 16)
            for r in range(2):
                sp.wait_ge(out_ready, r + 1)
                sp.dma_start(half(nodes(d.out), 1 - r), half(agg, 1 - r)).then_inc(stored, 16)
            sp.wait_ge(stored, 32)

        @block.gpsimd
        def _(pool):
            pool.wait_ge(w_in, 16 * 8)
            pool.wait_ge(x1_in, 16)
            nc.gpsimd.tensor_tensor(x1[:], x1[:], per_feature[:, 3, :].unsqueeze(1).to_broadcast([NP, NT, F]), ALU.add).then_inc(beta_added, 1)

        @block.vector
        def _(dve):
            count = [0]

            def link(ins):
                count[0] += 1
                ins.then_inc(done, 1)
                dve.wait_ge(done, count[0])

            link(nc.vector.tensor_scalar(per_count[:], d.cnt[:], AGG_EPS, None, ALU.add))
            link(nc.vector.reciprocal(per_count[:], per_count[:]))
            dve.wait_ge(w_in, 16 * 8)

            def add_biases(t):
                dve.wait_ge(prod_ready, t + 1)
                nc.vector.scalar_tensor_tensor(biased[:, t % 2, :], per_feature[:, 0, :], d.cnt_src[:, t:t + 1], prod[t % B][0:NP, 0:F],
                                               ALU.mult, ALU.add).then_inc(prod_used, 1)

            for r in range(2):
                for t in range(r * HT, (r + 1) * HT):
                    add_biases(t)
                    dve.wait_ge(prod_used, t + 1)
                    nc.vector.scalar_tensor_tensor(agg[:, t, :], per_feature[:, 1, :], d.cnt_dst[:, t:t + 1], biased[:, t % 2, :],
                                                   ALU.mult, ALU.add).then_inc(agg_ready, 1)
                    dve.wait_ge(agg_ready, t + 1)
                    nc.vector.scalar_tensor_tensor(leaky[:, t % 2, :], agg[:, t, :], SLOPE, agg[:, t, :], ALU.mult, ALU.max).then_inc(leaky_ready, 1)
                    dve.wait_ge(leaky_ready, t + 1)
                    if t == 0:
                        dve.wait_ge(h1_in, 16)
                    nc.vector.scalar_tensor_tensor(agg[:, t, :], leaky[:, t % 2, :], per_count[:, t:t + 1], h1[:, t, :], ALU.mult, ALU.add,
                                                   accum_out=stat[:, 0, t:t + 1]).then_inc(sum_ready, 1)
                dve.wait_ge(sum_ready, HT * (r + 1))
                here = slice(r * HT, (r + 1) * HT)
                nc.vector.tensor_scalar(stat[:, 0, here], stat[:, 0, here], -1.0 / F, None, ALU.mult).then_inc(mean_ready, 1)
            dve.wait_ge(squared, NT)
            nc.vector.tensor_scalar(stat[:, 1, :], stat[:, 1, :], 1.0 / F, LN_EPS, ALU.mult, ALU.add).then_inc(var_ready, 1)
            dve.wait_ge(std_ready, 1)
            link(nc.vector.reciprocal(stat[:, 1, :], stat[:, 2, :]))
            dve.wait_ge(mean_ready, 2)
            nc.vector.tensor_tensor(stat[:, 0, :], stat[:, 0, :], stat[:, 1, :], ALU.mult).then_inc(scale_ready, 1)
            dve.wait_ge(beta_added, 1)
            dve.wait_ge(scale_ready, 1)
            for t in range(HT, NT):
                last = nc.vector.tensor_scalar(agg[:, t, :], agg[:, t, :], stat[:, 1, t:t + 1], stat[:, 0, t:t + 1], ALU.mult, ALU.add)
            link(last)
            for n, r in enumerate((1, 0)):
                if r == 0:
                    dve.wait_ge(normed, HT)
                nc.vector.tensor_tensor(half(agg, r), half(agg, r), per_feature[:, 2, :].unsqueeze(1).to_broadcast([NP, HT, F]), ALU.mult).then_inc(scaled, 1)
                dve.wait_ge(scaled, n + 1)
                nc.vector.tensor_tensor(half(agg, r), half(agg, r), half(x1, r), ALU.add).then_inc(out_ready, 1)

        @block.tensor
        def _(pe):
            def turn(t):
                if t >= NT:
                    return
                if t >= 2:
                    pe.wait_ge(turn_copied, t - 1)
                nc.tensor.transpose(turned[t % 2][:, 0:NP], d.src_attr[:, t, :], d.ident[0:NP, 0:NP]).then_inc(turn_ready, 1)

            turn(0)
            pe.wait_ge(w_in, 16 * 8)
            for t in range(NT):
                turn(t + 1)
                if t >= B:
                    pe.wait_ge(prod_used, t - B + 1)
                out = prod[t % B][0:NP, 0:F]
                nc.tensor.matmul(out, d.src_sums[:, t:N:NT], w[:, 1, :], start=True, stop=False)
                nc.tensor.matmul(out, d.attr_by_dst[:, t:N:NT], w[:, 2, :], start=False, stop=False)
                if t == 0:
                    pe.wait_ge(row_in, 16)
                nc.tensor.matmul(out, row_sums[:, t:N:NT], w[:, 3, :], start=False, stop=False)
                pe.wait_ge(turn_copied, t + 1)
                nc.tensor.matmul(out, turn_sb[:, t % 2, :], w[:, 0, :], start=False, stop=True).then_inc(prod_ready, 1)

        @block.scalar
        def _(act):
            def square(t):
                act.wait_ge(mean_ready, t // HT + 1)
                if t >= 2:
                    act.wait_ge(squared, t - 1)
                nc.scalar.activation(squares[:, t % 2, :], agg[:, t, :], ACT.Square, bias=stat[:, 0, t:t + 1],
                                     accum_out=stat[:, 1, t:t + 1]).then_inc(squared, 1)

            for t in range(NT):
                act.wait_ge(turn_ready, t + 1)
                if t >= 2:
                    act.wait_ge(prod_ready, t - 1)
                nc.scalar.copy(turn_sb[:, t % 2, :], turned[t % 2][:, 0:NP]).then_inc(turn_copied, 1)
                if t >= SKEW:
                    square(t - SKEW)
            for t in range(NT - SKEW, NT):
                square(t)
            act.wait_ge(var_ready, 1)
            nc.scalar.activation(stat[:, 2, :], stat[:, 1, :], ACT.Sqrt).then_inc(std_ready, 1)
            act.wait_ge(scale_ready, 1)
            for t in range(HT):
                nc.scalar.activation(agg[:, t, :], agg[:, t, :], ACT.Identity, bias=stat[:, 0, t:t + 1], scale=stat[:, 1, t:t + 1]).then_inc(normed, 1)


def program(nc, d):
    dram = lambda name, shape, dt=F32: nc.dram_tensor(name, shape, dt).ap()
    d.src_i, d.dst_i = dram("src_pad", (EP,), I32), dram("dst_pad", (EP,), I32)
    d.src_f, d.dst_f = dram("src_float", (EP,)), dram("dst_float", (EP,))
    d.src_key, d.dst_key, d.dst_offset = dram("src_key", (EP,), I16), dram("dst_key", (EP,), I16), dram("dst_offset", (EP,), BF16)
    d.w_f = dram("w_pad", (EP,))
    d.rec = dram("edge_records", (NG, P, REC * J))
    d.g, d.h1, d.x1 = dram("g", (ROWS, F)), dram("h1", (ROWS, F)), dram("x1", (ROWS, F))
    d.agg, d.count_dst = dram("agg", (ROWS, F)), dram("count_dst", (N,))
    d.near = dram("near", (NEAR, SLOTS))
    d.attr_t, d.row_t, d.src_t = dram("attr_sums_t", (F, ROWS)), dram("row_sums_t", (F, ROWS)), dram("src_sums_t", (F, ROWS))
    d.tab_gcn = [dram(f"gcn_sums{k}", (ROWS, 2 * F)) for k in range(K)]
    d.tab_rows = [dram(f"row_sums{k}", (ROWS, F)) for k in range(K)]
    d.tab_dst = [dram(f"dst_sums{k}", (ROWS, 2 * F)) for k in range(K)]
    with ExitStack() as ctx:
        sb = lambda name, shape, dt=F32: ctx.enter_context(nc.sbuf_tensor(name, shape, dt))
        d.dinv = sb("dinv", [NP, NT])
        d.cnt = sb("cnt", [NP, NT])
        d.cnt_src, d.cnt_dst = sb("cnt_src", [NP, NT]), sb("cnt_dst", [NP, NT])
        d.ident = sb("ident", [P, P])
        d.ones = sb("ones", [P, P])
        d.iota = sb("iota", [P, P])
        d.part_i = sb("part_i", [P, J], I32)
        d.part = sb("part", [P, J])
        d.before_me = sb("before_me", [P, P])
        d.spare = sb("spare", [P, J])
        d.base_i = sb("base_i", [1, NG], I32)
        d.windowed = sb("windowed", [1, 1], I32)
        d.dense = sb("dense", [1, 1], I32)
        d.lo = sb("lo", [P, SUPER, PAIRS], BF16)
        d.hi = sb("hi", [P, SUPER, PAIRS], BF16)
        d.bank = [ctx.enter_context(nc.psum_tensor(f"bank{b}", [P, 512], F32)) for b in range(8)]
        with nc.sbuf_tensor("attr_sums", [F, ROWS], F32) as d.attr_sums:
            setup_and_degrees(nc, d)
            windowed = nc.values_load(d.windowed[0:1, 0:1], min_val=0, max_val=1)
            with nc.If(windowed == 1):
                edge_pass(nc, d, "gw", d.g, None, 0, d.tab_gcn, weighted=True, attr=True, window_sums=True)
            with nc.Else():
                edge_pass(nc, d, "gg", d.g, d.dst_i, 0, d.tab_gcn, weighted=True, attr=True)
            gcn_nodes(nc, d)
        with ExitStack() as inner:
            wide = lambda name, shape: inner.enter_context(nc.sbuf_tensor(name, shape, F32))
            d.src_sums = wide("src_sums", [F, TILES * P])
            d.src_attr = wide("src_attr", [NP, NT, F])
            d.attr_by_dst = wide("attr_by_dst", [F, TILES * P])
            HT = NT // 2
            d.src_attr_half = lambda h: d.src_attr[:, h * HT:(h + 1) * HT, :]
            d.part_half = lambda h: d.attr_by_dst[0:NP, h * HT * F:(h + 1) * HT * F].rearrange("p (t f) -> p t f", f=F)
            d.table_half = lambda k, h: d.tab_gcn[k][0:N, :].rearrange("(p t) f -> p t f", p=NP)[:, h * HT:(h + 1) * HT, F:2 * F]
            dense = nc.values_load(d.dense[0:1, 0:1], min_val=0, max_val=1)
            with nc.If(dense == 1):
                dense_sums(nc, d)
            with nc.Else():
                clear_tables(nc, d.tab_rows + d.tab_dst)
                edge_pass(nc, d, "rs", d.h1, d.dst_i, 0, d.tab_rows)
                edge_pass(nc, d, "rd", d.h1, d.src_i, 1, d.tab_dst, attr=True)
                turn_tables(nc, d, "by_src", d.tab_rows, (d.src_t,))
                turn_tables(nc, d, "by_dst", d.tab_dst, (d.row_t, d.attr_t))
                load_sums(nc, d)
            last_nodes(nc, d)


INPUTS = {"x": "x", "src": "src", "dst": "dst", "edge_attr_128": "edge_attr", "edge_weight": "w", "L0_gnn_kernel": "kernel",
          "L0_gnn_bias": "bias", "L1_gnn_W_fwd": "w_fwd", "L1_gnn_b_fwd": "b_fwd", "L1_gnn_W_back": "w_back",
          "L1_gnn_b_back": "b_back", "L1_gnn_gamma": "gamma", "L1_gnn_beta": "beta"}


def kernel(**inputs):
    import concourse.bacc as bacc
    from concourse.bass_utils import run_bass_kernel_spmd as run

    nc = bacc.Bacc("TRN2", target_bir_lowering=False, num_devices=1)
    d = Net()
    arrays = {}
    for name, short in INPUTS.items():
        a = np.ascontiguousarray(inputs[name])
        arrays[f"in_{name}"] = a
        d.__dict__[short] = nc.dram_tensor(f"in_{name}", a.shape, mybir.dt.from_np(a.dtype), kind="ExternalInput").ap()
    d.out = nc.dram_tensor("out", (N, F), F32, kind="ExternalOutput").ap()
    program(nc, d)
    return run(nc, [arrays], core_ids=[0]).results[0]["out"]
```
